# Optimizing a Trainium2 kernel written in Bass

```python
import numpy as np
import jax
import jax.numpy as jnp

def _softmax(x, axis=-1):
    return jax.nn.softmax(x, axis=axis)

def _gelu(x):
    return jax.nn.gelu(x, approximate=True)

def _silu(x):
    return jax.nn.silu(x)

def _sigmoid(x):
    return jax.nn.sigmoid(x)

def _layernorm(x, axis=-1, eps=1e-05):
    m = jnp.mean(x, axis=axis, keepdims=True)
    v = jnp.var(x, axis=axis, keepdims=True)
    return (x - m) / jnp.sqrt(v + eps)

def _scatter_add(tgt, idx, src, axis=0):
    return tgt.at[idx].add(src)

def _segment_sum(src, seg, n):
    return jax.ops.segment_sum(src, seg, n)
kernel_name = 'mk_xattn_ffn_d2_seqx_r4_950988'

def setup_inputs(seed: int=0):
    np.random.seed(seed)
    _w = jnp.asarray

    def _rec_inputs():
        import jax
        import jax.numpy as jnp
        _rk = jax.random.key(seed)
        x = -0.0003929 + 0.9999 * jax.random.normal(jax.random.fold_in(_rk, 1), (2, 1024, 256), jnp.float32)
        _lenS = 1024 - jax.random.randint(jax.random.fold_in(_rk, 7), (2,), 0, max(1, 1024 // 4) + 1, jnp.int32)
        _lenS2 = 64 - jax.random.randint(jax.random.fold_in(_rk, 8), (2,), 0, max(1, 64 // 4) + 1, jnp.int32)
        _ctx_768P = jax.random.normal(jax.random.fold_in(_rk, 11), (2, 16, 192), jnp.float32)
        _ctx_768c = jax.random.dirichlet(jax.random.fold_in(_rk, 511), 0.3 * jnp.ones((16,), jnp.float32), (2, 64))
        _ctx_768t = jnp.einsum('bsk,bkd->bsd', _ctx_768c, _ctx_768P)
        _ctx_768t = _ctx_768t * jax.lax.rsqrt(jnp.mean(jnp.square(_ctx_768t)) + 1e-12) * 0.953939
        ctx_768 = -0.00055796 + 0.999787 * (_ctx_768t + 0.3 * jax.random.normal(jax.random.fold_in(_rk, 611), (2, 64, 192), jnp.float32))
        return (x, ctx_768)
    x, ctx_768 = _rec_inputs()

    def _L0_xattn_setup():
        import jax, jax.numpy as jnp
        import numpy as np
        IMAGE_DIM = 256
        TEXT_DIM = 192
        NUM_HEADS = 16
        HEAD_DIM = IMAGE_DIM // NUM_HEADS
        key = jax.random.key(seed)
        ks = jax.random.split(key, 14)
        B, N, M = (4, 1024, 128)
        s_img = 1.0 / np.sqrt(IMAGE_DIM)
        s_txt = 1.0 / np.sqrt(TEXT_DIM)
        s_ff = 1.0 / np.sqrt(2 * IMAGE_DIM)
        return {'x': jax.random.normal(ks[0], (B, N, IMAGE_DIM), jnp.float32), 'y': jax.random.normal(ks[1], (B, M, TEXT_DIM), jnp.float32), 'Wq': jax.random.normal(ks[2], (IMAGE_DIM, IMAGE_DIM), jnp.float32) * s_img, 'bq': jax.random.normal(ks[3], (IMAGE_DIM,), jnp.float32) * s_img, 'Wk': jax.random.normal(ks[4], (TEXT_DIM, IMAGE_DIM), jnp.float32) * s_txt, 'bk': jax.random.normal(ks[5], (IMAGE_DIM,), jnp.float32) * s_txt, 'Wv': jax.random.normal(ks[6], (TEXT_DIM, IMAGE_DIM), jnp.float32) * s_txt, 'bv': jax.random.normal(ks[7], (IMAGE_DIM,), jnp.float32) * s_txt, 'W1': jax.random.normal(ks[8], (IMAGE_DIM, 2 * IMAGE_DIM), jnp.float32) * s_img, 'b1': jax.random.normal(ks[9], (2 * IMAGE_DIM,), jnp.float32) * s_img, 'W2': jax.random.normal(ks[10], (2 * IMAGE_DIM, IMAGE_DIM), jnp.float32) * s_ff, 'b2': jax.random.normal(ks[11], (IMAGE_DIM,), jnp.float32) * s_ff}
    _L0_xattn_all = _L0_xattn_setup()
    _L0_xattn_in = {k: v for k, v in _L0_xattn_all.items() if k in ('Wq', 'bq', 'Wk', 'bk', 'Wv', 'bv', 'W1', 'b1', 'W2', 'b2')}
    del _L0_xattn_all

    def _L0_ffn_setup():
        import jax, jax.numpy as jnp
        import numpy as np
        B, S, D_MODEL, D_FF, E, R, TOP_K = (4, 512, 256, 1024, 8, 16, 2)
        key = jax.random.key(seed)
        ks = jax.random.split(key, 9)
        sd = 1.0 / np.sqrt(D_MODEL)
        return {'hidden_states': jax.random.normal(ks[0], (B, S, D_MODEL), jnp.float32), 'wi': jax.random.normal(ks[1], (D_FF, D_MODEL), jnp.float32) * sd, 'bi': jax.random.normal(ks[2], (D_FF,), jnp.float32) * 0.01, 'wo': jax.random.normal(ks[3], (D_MODEL, D_FF), jnp.float32) * (1.0 / np.sqrt(D_FF)), 'bo': jax.random.normal(ks[4], (D_MODEL,), jnp.float32) * 0.01, 'lora_A': jax.random.normal(ks[5], (E, R, D_MODEL), jnp.float32) * sd, 'lora_B': jax.random.normal(ks[6], (E, D_FF, R), jnp.float32) * 0.02, 'gate_w': jax.random.normal(ks[7], (E, D_MODEL), jnp.float32) * sd, 'gate_b': jax.random.normal(ks[8], (E,), jnp.float32) * 0.01}
    _L0_ffn_all = _L0_ffn_setup()
    _L0_ffn_in = {k: v for k, v in _L0_ffn_all.items() if k in ('wi', 'bi', 'wo', 'bo', 'lora_A', 'lora_B', 'gate_w', 'gate_b')}
    del _L0_ffn_all

    def _L1_xattn_setup():
        import jax, jax.numpy as jnp
        import numpy as np
        B, LQ, LK = (4, 512, 512)
        D1, D2, H = (256, 192, 256)
        key = jax.random.key(seed)
        ks = jax.random.split(key, 9)
        s1, s2, sh = (1.0 / np.sqrt(D1), 1.0 / np.sqrt(D2), 1.0 / np.sqrt(H))
        return {'query': jax.random.normal(ks[0], (B, LQ, D1), jnp.float32), 'key': jax.random.normal(ks[1], (B, LK, D2), jnp.float32), 'value': jax.random.normal(ks[2], (B, LK, D2), jnp.float32), 'Wq': jax.random.normal(ks[3], (D1, H), jnp.float32) * s1, 'bq': jax.random.normal(ks[4], (H,), jnp.float32) * s1, 'Wk': jax.random.normal(ks[5], (D2, H), jnp.float32) * s2, 'bk': jax.random.normal(ks[6], (H,), jnp.float32) * s2, 'Wv': jax.random.normal(ks[7], (D2, H), jnp.float32) * s2, 'bv': jax.random.normal(ks[8], (H,), jnp.float32) * s2}
    _L1_xattn_all = _L1_xattn_setup()
    _L1_xattn_in = {k: v for k, v in _L1_xattn_all.items() if k in ('Wq', 'bq', 'Wk', 'bk', 'Wv', 'bv')}
    del _L1_xattn_all

    def _L1_ffn_setup():
        import jax, jax.numpy as jnp
        import numpy as np
        R = 64
        key = jax.random.key(seed)
        k1, k2, k3 = jax.random.split(key, 3)
        B, S, D_IN, D_OUT = (8, 1024, 256, 256)
        x = jax.random.normal(k1, (B, S, D_IN), dtype=jnp.float32)
        weight = jax.random.normal(k2, (D_OUT, D_IN), dtype=jnp.float32) * (1.0 / np.sqrt(D_IN))
        disha = jax.random.normal(k3, (R, D_OUT), dtype=jnp.float32) * 0.01
        return {'x': x, 'weight': weight, 'disha': disha}
    _L1_ffn_all = _L1_ffn_setup()
    _L1_ffn_in = {k: v for k, v in _L1_ffn_all.items() if k in ('weight', 'disha')}
    del _L1_ffn_all
    return {'x': x, 'ctx_768': ctx_768, 'L0_xattn_Wq': _L0_xattn_in['Wq'], 'L0_xattn_bq': _L0_xattn_in['bq'], 'L0_xattn_Wk': _L0_xattn_in['Wk'], 'L0_xattn_bk': _L0_xattn_in['bk'], 'L0_xattn_Wv': _L0_xattn_in['Wv'], 'L0_xattn_bv': _L0_xattn_in['bv'], 'L0_xattn_W1': _L0_xattn_in['W1'], 'L0_xattn_b1': _L0_xattn_in['b1'], 'L0_xattn_W2': _L0_xattn_in['W2'], 'L0_xattn_b2': _L0_xattn_in['b2'], 'L0_ffn_wi': _L0_ffn_in['wi'], 'L0_ffn_bi': _L0_ffn_in['bi'], 'L0_ffn_wo': _L0_ffn_in['wo'], 'L0_ffn_bo': _L0_ffn_in['bo'], 'L0_ffn_lora_A': _L0_ffn_in['lora_A'], 'L0_ffn_lora_B': _L0_ffn_in['lora_B'], 'L0_ffn_gate_w': _L0_ffn_in['gate_w'], 'L0_ffn_gate_b': _L0_ffn_in['gate_b'], 'L1_xattn_Wq': _L1_xattn_in['Wq'], 'L1_xattn_bq': _L1_xattn_in['bq'], 'L1_xattn_Wk': _L1_xattn_in['Wk'], 'L1_xattn_bk': _L1_xattn_in['bk'], 'L1_xattn_Wv': _L1_xattn_in['Wv'], 'L1_xattn_bv': _L1_xattn_in['bv'], 'L1_ffn_weight': _L1_ffn_in['weight'], 'L1_ffn_disha': _L1_ffn_in['disha']}

def reference(x, ctx_768, L0_xattn_Wq, L0_xattn_bq, L0_xattn_Wk, L0_xattn_bk, L0_xattn_Wv, L0_xattn_bv, L0_xattn_W1, L0_xattn_b1, L0_xattn_W2, L0_xattn_b2, L0_ffn_wi, L0_ffn_bi, L0_ffn_wo, L0_ffn_bo, L0_ffn_lora_A, L0_ffn_lora_B, L0_ffn_gate_w, L0_ffn_gate_b, L1_xattn_Wq, L1_xattn_bq, L1_xattn_Wk, L1_xattn_bk, L1_xattn_Wv, L1_xattn_bv, L1_ffn_weight, L1_ffn_disha):
    import jax
    import jax.numpy as jnp

    def _L0_xattn_ref(x, y, Wq, bq, Wk, bk, Wv, bv, W1, b1, W2, b2):
        import jax, jax.numpy as jnp
        import numpy as np
        IMAGE_DIM = 256
        TEXT_DIM = 192
        NUM_HEADS = 16
        HEAD_DIM = IMAGE_DIM // NUM_HEADS
        B, N, _ = x.shape
        M = y.shape[1]
        q = (x @ Wq + bq).reshape(B, N, NUM_HEADS, HEAD_DIM)
        k = (y @ Wk + bk).reshape(B, M, NUM_HEADS, HEAD_DIM)
        v = (y @ Wv + bv).reshape(B, M, NUM_HEADS, HEAD_DIM)
        scale = 1.0 / np.sqrt(HEAD_DIM)
        scores = jnp.einsum('bnhd,bmhd->bhnm', q, k) * scale
        attn = jax.nn.softmax(scores, axis=-1)
        out = jnp.einsum('bhnm,bmhd->bnhd', attn, v).reshape(B, N, IMAGE_DIM)
        h = jax.nn.relu(out @ W1 + b1)
        return h @ W2 + b2

    def _L0_ffn_ref(hidden_states, wi, bi, wo, bo, lora_A, lora_B, gate_w, gate_b):
        import jax, jax.numpy as jnp
        import numpy as np
        B, S, D_MODEL, D_FF, E, R, TOP_K = (4, 512, 256, 1024, 8, 16, 2)
        logits = jnp.einsum('bsd,ed->bse', hidden_states, gate_w) + gate_b
        scores = jax.nn.softmax(logits, axis=-1)
        top_v, top_i = jax.lax.top_k(scores, TOP_K)
        val_sum = top_v.sum(axis=-1)
        out = jnp.zeros_like(hidden_states)
        for e in range(E):
            count = (top_i == e).sum(axis=-1).astype(hidden_states.dtype)
            gate = count * val_sum
            inter = jnp.einsum('bsd,fd->bsf', hidden_states, wi) + bi + jnp.einsum('bsr,fr->bsf', jnp.einsum('bsd,rd->bsr', hidden_states, lora_A[e]), lora_B[e])
            h = jax.nn.relu(inter)
            expert_out = jnp.einsum('bsf,df->bsd', h, wo) + bo
            out = out + gate[..., None] * expert_out
        return out

    def _L1_xattn_ref(query, key, value, Wq, bq, Wk, bk, Wv, bv):
        import jax, jax.numpy as jnp
        import numpy as np
        B, LQ, LK = (4, 512, 512)
        D1, D2, H = (256, 192, 256)
        q = jnp.einsum('bqd,dh->bqh', query, Wq) + bq
        k = jnp.einsum('bkd,dh->bkh', key, Wk) + bk
        v = jnp.einsum('bkd,dh->bkh', value, Wv) + bv
        scores = jnp.einsum('bqh,bkh->bqk', q, k)
        weights = jax.nn.softmax(scores, axis=-1)
        return jnp.einsum('bqk,bkh->bqh', weights, v)

    def _L1_ffn_ref(x, weight, disha):
        import jax, jax.numpy as jnp
        import numpy as np
        R = 64
        result = jnp.einsum('bsd,od->bso', x, weight)
        r = disha.shape[0]
        pooled = x.reshape(*x.shape[:-1], x.shape[-1] // r, r).sum(axis=-2)
        return result + pooled @ disha
    x = x + _L0_xattn_ref(_layernorm(x, axis=-1), ctx_768, L0_xattn_Wq, L0_xattn_bq, L0_xattn_Wk, L0_xattn_bk, L0_xattn_Wv, L0_xattn_bv, L0_xattn_W1, L0_xattn_b1, L0_xattn_W2, L0_xattn_b2)
    x = x + _L0_ffn_ref(_layernorm(x, axis=-1), L0_ffn_wi, L0_ffn_bi, L0_ffn_wo, L0_ffn_bo, L0_ffn_lora_A, L0_ffn_lora_B, L0_ffn_gate_w, L0_ffn_gate_b)
    x = x + _L1_xattn_ref(_layernorm(x, axis=-1), ctx_768, ctx_768, L1_xattn_Wq, L1_xattn_bq, L1_xattn_Wk, L1_xattn_bk, L1_xattn_Wv, L1_xattn_bv)
    x = x + _L1_ffn_ref(_layernorm(x, axis=-1), L1_ffn_weight, L1_ffn_disha)
    return x

_drawn_inputs = setup_inputs


def setup_inputs(seed=0):
    import zlib

    import numpy as np

    out = dict(_drawn_inputs(seed))
    spreads = {}
    factors = {'L0_xattn_bq': 3.462,
     'L0_xattn_bk': 8.0,
     'L0_ffn_bi': 6.053,
     'L0_ffn_bo': 2.822,
     'L0_ffn_gate_b': 7.941,
     'L1_xattn_bk': 8.0}
    for name, (base, spread) in spreads.items():
        noise = np.random.default_rng([zlib.crc32(name.encode()), seed]).standard_normal(out[name].shape)
        drawn = base * np.exp(spread * noise) if base else spread * noise
        out[name] = jnp.asarray(drawn.astype(out[name].dtype))
    for name, factor in factors.items():
        out[name] = (out[name] * factor).astype(out[name].dtype)
    return out
```

```python
import numpy as np
import concourse.bass as bass
import concourse.mybir as mybir

F32 = mybir.dt.float32
F32R = mybir.dt.float32r
U32 = mybir.dt.uint32
ALU = mybir.AluOpType
ACT = mybir.ActivationFunctionType
AX = mybir.AxisListType

P = 128
BATCH, SEQ, D = 2, 1024, 256
KEYS, DC = 64, 192
HEADS = 16
HD = D // HEADS
F1 = 512
DFF, EXPERTS, RANK = 1024, 8, 16
T = 512
NT = T // P
NBLK = BATCH * SEQ // T
BPB = SEQ // T
KC = D // P
PAIRS = HEADS // 2
PW = 2 * HD
GPC = P // PW
CK = DC // 2
NF1 = F1 // P
NFF = DFF // P
GA = EXPERTS * RANK + EXPERTS
SROWS = 3 * PW + HEADS
EPS = 1e-5
SCALE = float(HD) ** -0.5

KV_A = PAIRS * P + KC * 512
KV_C = 2 * KC * KEYS + 2 * D


STAGED = ([("wq", 0), ("ga", 512), ("w1", 784)], [("w2", 0), ("lb", 1024)], [("wi", 0)], [("wo", 0)], [("wc", 0)])
SPLIT_ORDER = ["wq", "ga", "w1", "w2", "lb", "wi", "wo", "wc"]
STAGE_FREE = [0, 0, 3, 5, 6]
LATE = 6
A_SLOTS = [[("scores", 0), ("scores", 1)], [("scores", 2), ("scores", 3), ("attend", 0), ("attend", 1)],
           [("attend", 2), ("attend", 3), ("scores", 4), ("scores", 5)], [("scores", 6), ("scores", 7)],
           [("attend", 4), ("attend", 5), ("attend", 6), ("attend", 7)], [], [], []]


def build(nc, io):
    sb = lambda name, shape, dt=F32: nc.alloc_sbuf_tensor(name, [shape[0], int(np.prod(shape[1:]))], dt)
    sems = {}

    def sem(name):
        if name not in sems:
            sems[name] = nc.alloc_semaphore(name)
        return sems[name]

    def r3(t, a, lo=0, hi=None, rows=P):
        v = t[0:rows, lo:hi] if hi is not None else t[0:rows, lo:]
        return v.rearrange("p (a n) -> p a n", a=a)

    room = -(-nc.sbuf_base // 32) * 32
    hid_h = sb("hid_h", [P, NFF * T], F32R)
    hid_l = sb("hid_l", [P, NFF * T], F32R)
    xtf_h, xtf_l = sb("xtf_h", [P, KC * T], F32R), sb("xtf_l", [P, KC * T], F32R)
    at_h, at_l = sb("at_h", [P, 2 * T], F32R), sb("at_l", [P, 2 * T], F32R)
    xo = sb("xo", [P, NT * D])
    r1 = sb("r1", [P, 3 * T])
    ex = sb("ex", [P, 4 * T])
    hs32 = sb("hs32", [P, 2 * T])
    room_end = nc.sbuf_base
    HH, HL = r3(hid_h, NFF), r3(hid_l, NFF)

    widths = {"wq": KC * D, "ga": KC * GA, "w1": KC * F1, "w2": NF1 * D, "lb": DFF, "wi": KC * DFF, "wo": NFF * D,
              "wc": KC * D}
    chunks = {"wq": KC, "ga": KC, "w1": KC, "w2": NF1, "lb": 1, "wi": KC, "wo": NFF, "wc": KC}
    wh = {n: sb(n + "_h", [P, w], F32R) for n, w in widths.items()}
    wl = {n: sb(n + "_l", [P, w], F32R) for n, w in widths.items()}
    WH = {n: r3(wh[n], chunks[n]) for n in widths}
    WL = {n: r3(wl[n], chunks[n]) for n in widths}

    small = {}

    def const(name, cols, rows=P):
        small[name] = sb(name, [rows, cols])
        return small[name]

    ident = const("ident", P)
    eid = const("eid", P)
    ones_pair = const("ones_pair", PW)
    cols = const("cols", 20)
    nbi = const("nbi", NFF)
    b2row = const("b2row", D)
    gbrow = const("gbrow", EXPERTS)
    crow = const("crow", D)
    mhalf = const("mhalf", NT)
    BQ, B1, BI, BK0, BK1, BQ1 = 0, 2, 6, 14, 16, 18

    xta_h, xta_l = sb("xta_h", [P, KC * T], F32R), sb("xta_l", [P, KC * T], F32R)
    XTA = (r3(xta_h, KC), r3(xta_l, KC))
    XTF = (r3(xtf_h, KC), r3(xtf_l, KC))
    qo_h, qo_l = sb("qo_h", [P, KC * T], F32R), sb("qo_l", [P, KC * T], F32R)
    QO = (r3(qo_h, KC), r3(qo_l, KC))
    AT = (r3(at_h, 2), r3(at_l, 2))
    stack = sb("stack", [P, PAIRS * T], F32R)
    QS = r3(stack, PAIRS, rows=SROWS)
    HS = (r3(stack, 2 * NF1)[:, 0:NF1, :], r3(stack, 2 * NF1)[:, NF1:, :])
    mxT = sb("mxT", [HEADS, T], F32R)
    kva = sb("kva", [P, KV_A], F32R)
    KS = r3(kva, PAIRS, 0, PAIRS * P, rows=SROWS)
    KBH = r3(kva, KC, PAIRS * P, KV_A)
    kvc = sb("kvc", [P, KV_C], F32R)
    G = (r3(kvc, KC, 0, KC * KEYS), r3(kvc, KC, KC * KEYS, 2 * KC * KEYS))
    V1 = (kvc[:, 2 * KC * KEYS:2 * KC * KEYS + D], kvc[:, 2 * KC * KEYS + D:KV_C])
    vcur = sb("vcur", [P, D])
    gbcur = sb("gbcur", [P, KEYS])

    xin, xmid = sb("xin", [P, NT * D]), sb("xmid", [P, NT * D])
    XIN, XMID, XO = r3(xin, NT), r3(xmid, NT), r3(xo, NT)
    xn = sb("xn", [P, NT * D])
    XN = r3(xn, NT)
    EX = r3(ex, 4)
    rec = sb("rec", [P, T])
    o32 = sb("o32", [P, T])
    HS32 = r3(hs32, 2)
    R1 = r3(r1, 3)
    mx = sb("mx", [P, NT * HEADS])
    MX = r3(mx, NT)
    lnst = {j: (sb(f"st{j}", [P, NT * 6]), sb(f"mv{j}", [P, NT * 3]), sb(f"ve{j}", [P, NT]), sb(f"nm{j}", [P, NT]),
                sb(f"rs{j}", [P, NT]), sb(f"nmr{j}", [P, NT])) for j in (1, 2, 3, 4)}
    lg, srt, srtd, srte = (sb(n, [P, NT * EXPERTS]) for n in ("lg", "srt", "srtd", "srte"))
    idx = sb("idx", [P, NT * EXPERTS], U32)
    idxf = sb("idxf", [P, NT * EXPERTS])
    gsum, grec, gnum, gate = (sb(n, [P, NT]) for n in ("gsum", "grec", "gnum", "gate"))
    am = r1
    sc1 = sb("sc1", [P, NT * KEYS])
    SC1 = r3(sc1, NT)
    mx1, sum1, rec1 = (sb(n, [P, NT]) for n in ("mx1", "sum1", "rec1"))
    tmpo = sb("tmpo", [P, D])


    place = [room]

    def temp(name, shape, dt=F32):
        n = int(np.prod(shape[1:]))
        t = nc.alloc_sbuf_tensor_at(name, [shape[0], n], dt, offset=place[0])
        place[0] += 4 * n
        assert place[0] <= room_end
        return t

    stage = (temp("stage_a", [P, 2048]), temp("stage_b", [P, 2048]))
    kb_h, kb_l = temp("kb_h", [P, BATCH * KC * 512], F32R), temp("kb_l", [P, BATCH * KC * 512], F32R)
    KB = (r3(kb_h, BATCH * KC), r3(kb_l, BATCH * KC))
    wq1t = temp("wq1t", [P, KC * D])
    kt0, kt1 = temp("kt0", [P, KC * P]), temp("kt1", [P, KC * P])
    kt0_h, kt0_l = temp("kt0_h", [P, KC * P], F32R), temp("kt0_l", [P, KC * P], F32R)
    bvrow0, bvrow1 = temp("bvrow0", [P, D]), temp("bvrow1", [P, D])
    vmask = temp("vmask", [P, D])
    g_h, g_l = temp("g_h", [P, KC * P], F32R), temp("g_l", [P, KC * P], F32R)
    v0 = temp("v0", [P, BATCH * D])
    v1, v1_h, v1_l = (temp(n, [P, BATCH * D], dt) for n, dt in (("v1", F32), ("v1_h", F32R), ("v1_l", F32R)))
    gb = temp("gb", [P, BATCH * KEYS])
    ind = temp("ind", [P, PAIRS * P])
    disha = temp("disha", [P, D])
    borow = temp("borow", [P, D])
    kmask = temp("kmask", [P, 8])
    kvw = {n: temp(n, [CK, 2 * D]) for n in ("wk0", "wv0", "wk1", "wv1")}
    ctx = temp("ctx", [CK, 2 * BATCH * KEYS])
    ctxd = temp("ctxd", [CK, 2 * BATCH * 2 * KEYS])

    kvr = nc.dram_tensor("kv_r", (BATCH, P, KV_A + KV_C), F32, kind="Internal").ap()
    kvf = nc.dram_tensor("kv_f", (BATCH, P, D + KEYS), F32, kind="Internal").ap()

    psT = nc.alloc_psum_tensor("psT", [P, 1024], F32)
    psI = nc.alloc_psum_tensor("psI", [P, 1536], F32)
    psS = nc.alloc_psum_tensor("psS", [P, 1024], F32)
    psP = nc.alloc_psum_tensor("psP", [P, 512], F32)
    T_, I_, S_ = (lambda k, t=t: t[:, 512 * k:512 * k + 512] for t in (psT, psI, psS))
    P0 = psP[:, :]

    as32 = lambda ap: ap.bitcast(F32)
    x_v = io["x"].rearrange("(b p t) d -> b p t d", p=P, t=NT)
    out_v = io["out"].rearrange("(b p t) d -> b p t d", p=P, t=NT)
    S = sem
    block = nc.Block()
    ibank = lambda f: (f + 2) % 3

    def after_first(eng, s, b, per):
        if not (isinstance(b, int) and b == 0):
            eng.wait_ge(s, b * per)

    with block:
        @block.sync
        def _(sp):
            small_loads = [(ctx[:, :], "ctx"), (ctxd[:, :], "ctxd"), (cols[:, :], "cols"), (kmask[:, :], "kmask"),
                           (ident[:, :], "ident"), (vmask[:, :], "vmask"), (bvrow0[:, :], "bvrow0"),
                           (bvrow1[:, :], "bvrow1")]
            sp.dma_start(kvw["wk0"][:, :], io["wk0"]).then_inc(S("ld_wk0"), 16)
            sp.dma_start(XIN, x_v[0]).then_inc(S("x_in"), 16)
            for dst, n in small_loads:
                sp.dma_start(dst, io[n]).then_inc(S("ld_small"), 16)
            for n in ("wv0", "wk1", "wv1"):
                sp.dma_start(kvw[n][:, :], io[n]).then_inc(S("ld_kvw"), 16)
            sp.dma_start(wq1t[:, :], io["wq1t"]).then_inc(S("ld_kvw"), 16)
            for n, at in STAGED[0]:
                sp.dma_start(stage[0][:, at:at + widths[n]], io[n]).then_inc(S("ld_" + n), 16)
            for n, at in STAGED[1]:
                sp.dma_start(stage[1][:, at:at + widths[n]], io[n]).then_inc(S("ld_" + n), 16)
            for dst, n in ((eid[:, :], "eid"), (ones_pair[:, :], "ones_pair"), (b2row[:, :], "b2row"),
                           (gbrow[:, :], "gbrow"), (disha[:, :], "disha"),
                           (ind[3 * PW:SROWS, :], "ind")):
                sp.dma_start(dst, io[n]).then_inc(S("ld_late"), 16)
            sp.dma_start(borow[:, :], io["borow"]).then_inc(S("stored"), 16)

            sp.wait_ge(S("kb_split"), 2 * BATCH * KC)
            for b in range(BATCH):
                for r, half in ((0, kb_h), (1, kb_h), (2, kb_l)):
                    for g in range(GPC):
                        src = half[PW * g:PW * g + PW, b * KC * 512:(b + 1) * KC * 512].rearrange(
                            "p (m n) -> p m n", m=KC)[:, :, g * P:(g + 1) * P]
                        dst = kvr[b, PW * r:PW * r + PW, 0:PAIRS * P].rearrange(
                            "p (m g n) -> p m g n", m=KC, g=GPC)[:, :, g, :]
                        sp.dma_start(dst, as32(src)).then_inc(S("kv_stored"), 16)
                sp.dma_start(kvr[b, :, PAIRS * P:KV_A], as32(kb_h[:, b * KC * 512:(b + 1) * KC * 512])).then_inc(
                    S("kv_stored"), 16)
            sp.wait_ge(S("v0_ready"), BATCH)
            for b in range(BATCH):
                sp.dma_start(kvf[b, :, 0:D], v0[:, b * D:(b + 1) * D]).then_inc(S("kv_stored"), 16)

            def load_a(b):
                after_first(sp, S("pv"), b, PAIRS)
                bb = b // BPB
                sp.dma_start(as32(kva[0:3 * PW, 0:PAIRS * P]), kvr[bb, 0:3 * PW, 0:PAIRS * P]).then_inc(S("kva"), 16)
                sp.dma_start(as32(kva[:, PAIRS * P:KV_A]), kvr[bb, :, PAIRS * P:KV_A]).then_inc(S("kva"), 16)
                sp.dma_start(vcur[:, :], kvf[bb, :, 0:D]).then_inc(S("kva"), 16)

            def load_c(b):
                sp.wait_ge(S("stored"), (b + 1) * 16)
                bb = b // BPB
                sp.dma_start(as32(kvc[:, :]), kvr[bb, :, KV_A:]).then_inc(S("kvc"), 16)
                sp.dma_start(gbcur[:, :], kvf[bb, :, D:]).then_inc(S("kvc"), 16)

            def load_x(b):
                sp.wait_ge(S("ln1_xh"), b * NT)
                sp.wait_ge(S("xres"), b)
                sp.dma_start(XIN, x_v[b]).then_inc(S("x_in"), 16)

            def stack_q(b):
                sp.wait_ge(S("qh"), (b + 1) * KC)
                sp.wait_ge(S("ql"), (b + 1) * KC)
                for r, half in ((0, 0), (1, 1), (2, 0)):
                    for g in range(GPC):
                        dst = stack[PW * r:PW * r + PW, :].rearrange("p (m g n) -> p m g n", m=KC, g=GPC)[:, :, g, :]
                        sp.dma_start(as32(dst), as32(QO[half][PW * g:PW * g + PW, :, :])).then_inc(S("qstack"), 16)

            def stack_m(b):
                sp.wait_ge(S("mxT"), b + 1)
                sp.dma_start(as32(r3(stack, PAIRS)[3 * PW:SROWS, :, :]),
                             as32(mxT[:, :]).unsqueeze(1).broadcast_to([HEADS, PAIRS, T])).then_inc(S("mstack"), 16)

            sp.wait_ge(S("kv_stored"), 16 * BATCH * (3 * GPC + 2))
            load_a(0)
            stack_q(0)
            stack_m(0)
            sp.wait_ge(S("g_ready"), 2)
            sp.wait_ge(S("v1_ready"), 2)
            sp.wait_ge(S("gb_ready"), 1)
            for b in range(BATCH):
                for hl, (gt, vt) in enumerate(((g_h, v1_h), (g_l, v1_l))):
                    o = KV_A + hl * KC * KEYS
                    sp.dma_start(kvr[b, :, o:o + KC * KEYS].rearrange("p (m n) -> p m n", m=KC),
                                 as32(gt[:, :]).rearrange("p (m b n) -> p m b n", m=KC, b=BATCH)[:, :, b, :]).then_inc(
                        S("kvc_stored"), 16)
                    o = KV_A + 2 * KC * KEYS + hl * D
                    sp.dma_start(kvr[b, :, o:o + D], as32(vt[:, b * D:(b + 1) * D])).then_inc(S("kvc_stored"), 16)
                sp.dma_start(kvf[b, :, D:], gb[:, b * KEYS:(b + 1) * KEYS]).then_inc(S("kvc_stored"), 16)
            load_x(1)
            for half in (0, 1, 2):
                for n, at in STAGED[2 + half]:
                    sp.wait_ge(S("split_l"), STAGE_FREE[2 + half])
                    sp.dma_start(stage[half % 2][:, at:at + widths[n]], io[n]).then_inc(S("ld_" + n), 16)
            sp.wait_ge(S("kvc_stored"), 16 * BATCH * 5)

            with sp.Fori(1, NBLK - 1) as i:
                load_a(i)
                stack_q(i)
                stack_m(i)
                load_c(i - 1)
                load_x(i + 1)
            load_a(NBLK - 1)
            stack_q(NBLK - 1)
            stack_m(NBLK - 1)
            load_c(NBLK - 2)
            load_c(NBLK - 1)
            sp.wait_ge(S("stored"), 16 * (NBLK + 1))

        @block.tensor
        def _(pe):
            mm = nc.tensor.matmul

            def three(out, lhs, rhs, chunks, start=True, stop=True, **kw):
                n = len(chunks)
                for q, (a, b) in enumerate(((0, 0), (1, 0), (0, 1))):
                    for k, c in enumerate(chunks):
                        last = mm(out, lhs(a, c), rhs(b, c), start=start and q == 0 and k == 0,
                                  stop=stop and q == 2 and k == n - 1, **kw)
                return last

            def w(name, m, n=P):
                return lambda a, c: (WH, WL)[a][name][:, c, m:m + n]

            def x_of(pair, lo=0, n=T):
                return lambda a, c: pair[a][:, c, lo:lo + n]

            def transposes(j, b):
                for c in range(KC):
                    for t in range(NT):
                        pe.wait_ge(S(f"ln{j}_xh"), b * NT + t + 1)
                        last = nc.tensor.transpose(T_(c)[:, t * P:(t + 1) * P], XN[:, t, c * P:(c + 1) * P], ident[:, :])
                    last.then_inc(S(f"ln{j}_T"), 1)

            def a_queries(b, m):
                pe.wait_ge(S("ln1_h"), (b + 1) * KC)
                pe.wait_ge(S("ln1_l"), (b + 1) * KC)
                three(S_(m), w("wq", m * P), x_of(XTA), range(KC)).then_inc(S("q_ps"), 1)

            def a_row_scores(b, t):
                pe.wait_ge(S("kva"), (b + 1) * 48)
                pe.wait_ge(S("qh"), (b + 1) * KC)
                if t == 0:
                    pe.wait_ge(S("ql"), (b + 1) * KC)
                else:
                    pe.wait_ge(S("mx"), b * NT + t)
                for m in range(KC):
                    last = mm(S_(m), QO[0][:, m, t * P:(t + 1) * P], KBH[:, m, :], start=True, stop=True)
                last.then_inc(S("row_sc"), 1)

            def a_max_transposes(b):
                pe.wait_ge(S("mx"), (b + 1) * NT)
                for t in range(NT):
                    last = nc.tensor.transpose(P0[0:HEADS, t * P:(t + 1) * P], MX[:, t, :], ident[:, :])
                last.then_inc(S("mxT_ps"), 1)

            def a_scores(b, c):
                pe.wait_ge(S("qstack"), (b + 1) * 16 * 3 * GPC)
                pe.wait_ge(S("mstack"), (b + 1) * 16)
                if c >= 2:
                    pe.wait_ge(S("ex"), b * PAIRS + c - 1)
                mm(S_(c % 2), KS[:, c, :], QS[:, c, :], start=True, stop=True).then_inc(S("sc"), 1)

            def a_attend(b, c):
                g = c % GPC
                pe.wait_ge(S("ex"), b * PAIRS + c + 1)
                if c == GPC:
                    pe.wait_ge(S("o32"), b * KC + 1)
                mm(T_(0)[PW * g:PW * g + PW, :], vcur[:, c * PW:(c + 1) * PW], EX[:, c % 4, :], start=True, stop=True)
                mm(T_(1)[PW * g:PW * g + PW, :], ones_pair[:, :], EX[:, c % 4, :], start=True, stop=True).then_inc(
                    S("pv"), 1)

            def a_hidden(b, f):
                pe.wait_ge(S("oh"), (b + 1) * KC)
                pe.wait_ge(S("ol"), (b + 1) * KC)
                if f >= 2:
                    pe.wait_ge(S("hs"), b * NF1 + f - 1)
                three(S_(f % 2), w("w1", f * P), x_of(QO), range(KC)).then_inc(S("hs_ps"), 1)

            def a_out(b, half):
                pe.wait_ge(S("hsh"), (b + 1) * NF1)
                pe.wait_ge(S("hsl"), (b + 1) * NF1)
                bank = (P0, I_(2))[half]
                for t in (2 * half, 2 * half + 1):
                    last = three(bank[:, (t % 2) * D:(t % 2 + 1) * D], x_of(HS, t * P, P), w("w2", 0, D), range(NF1))
                last.then_inc(S("x1_ps"), 1)

            def f_gate(b, half):
                pe.wait_ge(S("ln2_h"), (b + 1) * KC)
                pe.wait_ge(S("ln2_l"), (b + 1) * KC)
                for t in (2 * half, 2 * half + 1):
                    o = (t % 2) * 256
                    last = three(I_(half)[:, o:o + GA], x_of(XTF, t * P, P), w("ga", 0, GA), range(KC))
                last.then_inc(S("ga_ps"), 1)

            def f_lora_transposes(b):
                for q in range(2):
                    pe.wait_ge(S("am"), b * 2 + q + 1)
                    for t in range(NT):
                        last = nc.tensor.transpose(T_(q)[:, t * P:(t + 1) * P],
                                                   r1[:, q * T + t * P:q * T + (t + 1) * P], ident[:, :])
                    last.then_inc(S("amT"), 1)

            def f_base(b, f):
                pe.wait_ge(S("ln2_l"), (b + 1) * KC)
                if f >= 3:
                    pe.wait_ge(S("hid"), b * NFF + f - 2)
                three(I_(ibank(f)), w("wi", f * P), x_of(XTF), range(KC), stop=False, skip_group_check=True)

            def f_first(b, f):
                pe.wait_ge(S("ath"), b * 2 + 1)
                pe.wait_ge(S("atl"), b * 2 + 1)
                lb = lambda a: (WH, WL)[a]["lb"][:, 0, f * P:(f + 1) * P]
                for q, (x, y) in enumerate(((0, 0), (1, 0), (0, 1))):
                    last = mm(I_(ibank(f)), lb(x), AT[y][:, 0, :], start=False, stop=q == 2, skip_group_check=True)
                last.then_inc(S("first_ps"), 1)

            def f_second(b, f):
                pe.wait_ge(S("ath"), b * 2 + 2)
                pe.wait_ge(S("atl"), b * 2 + 2)
                pe.wait_ge(S("r1"), b * NFF + f + 1)
                lb = lambda a: (WH, WL)[a]["lb"][:, 0, f * P:(f + 1) * P]
                for q, (x, y) in enumerate(((0, 0), (1, 0), (0, 1))):
                    last = mm(I_(ibank(f)), lb(x), AT[y][:, 1, :], start=False, stop=q == 2, skip_group_check=True)
                last.then_inc(S("second_ps"), 1)

            def f_out(b, half):
                pe.wait_ge(S("hidh"), (b + 1) * NFF)
                pe.wait_ge(S("hidl"), (b + 1) * NFF)
                for t in (2 * half, 2 * half + 1):
                    o = (t % 2) * D
                    last = three(I_(half)[:, o:o + D], x_of((HH, HL), t * P, P), w("wo", 0, D), range(NFF))
                last.then_inc(S("x2_ps"), 1)

            def c_scores(b):
                pe.wait_ge(S("kvc"), (b + 1) * 32)
                pe.wait_ge(S("ln3_h"), (b + 1) * KC)
                pe.wait_ge(S("ln3_l"), (b + 1) * KC)
                for t in range(NT):
                    last = three(S_(0)[:, t * KEYS:(t + 1) * KEYS], x_of(XTF, t * P, P), x_of(G, 0, KEYS), range(KC))
                last.then_inc(S("sc1_ps"), 1)

            def c_transposes(b):
                pe.wait_ge(S("ex1"), b + 1)
                for u in range(NT // 2):
                    last = nc.tensor.transpose(S_(1)[:, u * P:(u + 1) * P], sc1[:, u * P:(u + 1) * P], ident[:, :])
                last.then_inc(S("ex1T"), 1)

            def c_attend(b, odd):
                pe.wait_ge(S("eh"), b + 1)
                pe.wait_ge(S("el"), b + 1)
                rows = slice(odd * KEYS, (odd + 1) * KEYS)
                for u in range(NT // 2):
                    for q, (x, y) in enumerate(((0, 0), (1, 0), (0, 1))):
                        last = mm(I_(odd)[:, u * D:(u + 1) * D], AT[x][rows, 0, u * P:(u + 1) * P], V1[y][rows, :],
                                  start=q == 0, stop=q == 2)
                last.then_inc(S("p1"), 1)

            def d_linear(b, half):
                pe.wait_ge(S("ln4_h"), (b + 1) * KC)
                pe.wait_ge(S("ln4_l"), (b + 1) * KC)
                for t in (2 * half, 2 * half + 1):
                    o = (t % 2) * D
                    last = three(I_(half)[:, o:o + D], x_of(XTF, t * P, P), w("wc", 0, D), range(KC))
                last.then_inc(S("x4_ps"), 1)

            pe.wait_ge(S("ld_wk0"), 16)
            pe.wait_ge(S("ld_small"), 16 * 8)
            pe.wait_ge(S("ld_kvw"), 16 * 4)
            for n, bank in (("wk0", 0), ("wk1", 1)):
                for m in range(KC):
                    for k in range(2):
                        last = mm(I_(bank)[:, m * P:(m + 1) * P], kvw[n][:, k * D + m * P:k * D + (m + 1) * P],
                                  ctx[:, k * P:(k + 1) * P], start=k == 0, stop=k == 1)
                last.then_inc(S("kt_ps"), 1)
            for b in range(BATCH):
                for k in range(2):
                    o = k * 2 * P + b * P
                    last = mm(I_(2)[:, b * D:(b + 1) * D], ctxd[:, o:o + P], kvw["wv0"][:, k * D:(k + 1) * D],
                              start=k == 0, stop=k == 1)
            last.then_inc(S("v0_ps"), 1)
            for b in range(BATCH):
                for k in range(2):
                    o = k * 2 * P + b * P
                    last = mm(P0[:, b * D:(b + 1) * D], ctxd[:, o:o + P], kvw["wv1"][:, k * D:(k + 1) * D],
                              start=k == 0, stop=k == 1)
            last.then_inc(S("v1_ps"), 1)

            def body(a, f, h):
                if f is not None:
                    transposes(2, f)
                if a is not None:
                    a_row_scores(a, 0)
                if f is not None:
                    f_gate(f, 0)
                if a is not None:
                    a_row_scores(a, 1)
                if f is not None:
                    f_gate(f, 1)
                if a is not None:
                    a_row_scores(a, 2)
                if f is not None:
                    f_base(f, 0)
                if a is not None:
                    a_row_scores(a, 3)
                if f is not None:
                    f_lora_transposes(f)
                if a is not None:
                    a_max_transposes(a)
                for s in range(NFF):
                    if f is not None:
                        f_first(f, s)
                        if s + 1 < NFF:
                            f_base(f, s + 1)
                        f_second(f, s)
                    if a is not None:
                        for kind, c in A_SLOTS[s]:
                            (a_scores if kind == "scores" else a_attend)(a, c)
                if a is not None:
                    a_hidden(a, 0)
                    a_hidden(a, 1)
                if f is not None:
                    f_out(f, 0)
                    f_out(f, 1)
                if a is not None:
                    a_hidden(a, 2)
                    a_hidden(a, 3)
                    a_out(a, 0)
                if f is not None:
                    transposes(3, f)
                if a is not None:
                    a_out(a, 1)
                if f is not None:
                    c_scores(f)
                if h is not None:
                    transposes(1, h)
                if f is not None:
                    c_transposes(f)
                if h is not None:
                    a_queries(h, 0)
                if f is not None:
                    c_attend(f, 0)
                    c_attend(f, 1)
                if h is not None:
                    a_queries(h, 1)
                if f is not None:
                    transposes(4, f)
                    d_linear(f, 0)
                    d_linear(f, 1)

            pe.wait_ge(S("ld_small"), 16 * 8)
            transposes(1, 0)
            pe.wait_ge(S("split_h"), 1)
            pe.wait_ge(S("split_l"), 1)
            a_queries(0, 0)
            a_queries(0, 1)
            pe.wait_ge(S("kt"), 2)
            for m in range(KC):
                for k in range(KC):
                    last = mm(I_(0)[:, m * P:(m + 1) * P], wq1t[:, k * D + m * P:k * D + (m + 1) * P],
                              kt1[:, k * P:(k + 1) * P], start=k == 0, stop=k == 1)
            last.then_inc(S("g_ps"), 1)
            for k in range(KC):
                last = mm(I_(1)[:, 0:P], cols[:, BQ1 + k:BQ1 + k + 1].broadcast_to([P, P]), kt1[:, k * P:(k + 1) * P],
                          start=k == 0, stop=k == 1)
            last.then_inc(S("gb_ps"), 1)
            pe.wait_ge(S("ld_late"), 16 * LATE)
            pe.wait_ge(S("ind"), 1)
            pe.wait_ge(S("split_h"), 4)
            pe.wait_ge(S("split_l"), 4)
            body(0, None, 1)
            pe.wait_ge(S("ld_wo"), 16)
            pe.wait_ge(S("gb_ready"), 1)
            for f in range(NFF):
                last = mm(I_(1)[:, 0:D], cols[:, BI + f:BI + f + 1].broadcast_to([P, P]),
                          stage[1][:, f * D:(f + 1) * D], start=f == 0, stop=f == NFF - 1)
            last.then_inc(S("crow_ps"), 1)
            pe.wait_ge(S("crow"), 1)
            pe.wait_ge(S("split_h"), len(SPLIT_ORDER))
            pe.wait_ge(S("split_l"), len(SPLIT_ORDER))
            with pe.Fori(1, NBLK - 1) as i:
                body(i, i - 1, i + 1)
            body(NBLK - 1, NBLK - 2, None)
            body(None, NBLK - 1, None)

        @block.scalar
        def _(act):
            A = nc.scalar.activation

            def normalise(j, b, src):
                act.wait_ge(S(f"ln{j}_nmr"), b + 1)
                for t in range(NT):
                    A(XN[:, t, :], src[:, t, :], ACT.Identity, scale=lnst[j][4][:, t:t + 1],
                      bias=lnst[j][5][:, t:t + 1]).then_inc(S(f"ln{j}_xh"), 1)

            def high(j, b, dst):
                for c in range(KC):
                    act.wait_ge(S(f"ln{j}_T"), b * KC + c + 1)
                    A(dst[0][:, c, :], T_(c), ACT.Identity).then_inc(S(f"ln{j}_h"), 1)

            def queries(b, m):
                act.wait_ge(S("q_ps"), b * KC + m + 1)
                A(QO[0][:, m, :], S_(m), ACT.Identity, bias=cols[:, BQ + m:BQ + m + 1]).then_inc(S("qh"), 1)

            def head(b):
                normalise(1, b, XIN)
                high(1, b, XTA)

            def maxima(b):
                act.wait_ge(S("mxT_ps"), b + 1)
                if not (isinstance(b, int) and b == 0):
                    act.wait_ge(S("mstack"), b * 16)
                A(mxT[:, :], P0[0:HEADS, :], ACT.Identity).then_inc(S("mxT"), 1)

            def exps(b, c):
                act.wait_ge(S("sc"), b * PAIRS + c + 1)
                if c >= 4:
                    act.wait_ge(S("pv"), b * PAIRS + c - 3)
                A(EX[:, c % 4, :], S_(c % 2), ACT.Exp, scale=SCALE).then_inc(S("ex"), 1)

            def attended(b, m):
                act.wait_ge(S("o32"), b * KC + m + 1)
                A(QO[0][:, m, :], o32[:, :], ACT.Identity).then_inc(S("oh"), 1)

            def hidden(b, f):
                act.wait_ge(S("hs_ps"), b * NF1 + f + 1)
                if f >= 2:
                    act.wait_ge(S("hsl"), b * NF1 + f - 1)
                A(HS32[:, f % 2, :], S_(f % 2), ACT.Relu, bias=cols[:, B1 + f:B1 + f + 1]).then_inc(S("hs"), 1)
                act.wait_ge(S("hs"), b * NF1 + f + 1)
                A(HS[0][:, f, :], HS32[:, f % 2, :], ACT.Identity).then_inc(S("hsh"), 1)

            def sorted_exps(b):
                act.wait_ge(S("srtd"), b + 1)
                A(srte[:, :], srtd[:, :], ACT.Exp).then_inc(S("srte"), 1)

            def lora_high(b):
                for q in range(2):
                    act.wait_ge(S("amT"), b * 2 + q + 1)
                    A(AT[0][:, q, :], T_(q), ACT.Identity).then_inc(S("ath"), 1)

            def first_relu(b, f):
                act.wait_ge(S("first_ps"), b * NFF + f + 1)
                if f >= 3:
                    act.wait_ge(S("hidl"), b * NFF + f - 2)
                A(R1[:, f % 3, :], I_(ibank(f)), ACT.Relu, bias=cols[:, BI + f:BI + f + 1]).then_inc(S("r1"), 1)

            def sum_high(b, f):
                act.wait_ge(S("hid"), b * NFF + f + 1)
                A(HH[:, f, :], R1[:, f % 3, :], ACT.Identity).then_inc(S("hidh"), 1)

            def weights_exp(b):
                act.wait_ge(S("sc1"), b + 1)
                A(sc1[:, :], sc1[:, :], ACT.Exp).then_inc(S("ex1"), 1)

            def weights_high(b):
                act.wait_ge(S("ex1T"), b + 1)
                A(AT[0][:, 0, 0:2 * P], S_(1)[:, 0:2 * P], ACT.Identity).then_inc(S("eh"), 1)

            def store(b):
                act.wait_ge(S("x4"), (b + 1) * NT)
                act.dma_start(out_v[b], XO).then_inc(S("stored"), 16)

            def body(a, f, h):
                if f is not None:
                    normalise(2, f, XMID)
                    high(2, f, XTF)
                    sorted_exps(f)
                    lora_high(f)
                if a is not None:
                    maxima(a)
                for s in range(NFF):
                    if f is not None:
                        first_relu(f, s)
                        if s >= 1:
                            sum_high(f, s - 1)
                    if a is not None:
                        for kind, c in A_SLOTS[s]:
                            if kind == "scores":
                                exps(a, c)
                        if s in (5, 6):
                            attended(a, s - 5)
                if f is not None:
                    sum_high(f, NFF - 1)
                if a is not None:
                    for c in range(NF1):
                        hidden(a, c)
                if f is not None:
                    normalise(3, f, XO)
                    high(3, f, XTF)
                if h is not None and f is not None:
                    normalise(1, h, XIN)
                if f is not None:
                    weights_exp(f)
                if h is not None:
                    if f is None:
                        normalise(1, h, XIN)
                    high(1, h, XTA)
                if f is not None:
                    weights_high(f)
                if h is not None:
                    queries(h, 0)
                    if f is None:
                        queries(h, 1)
                if f is not None:
                    normalise(4, f, XO)
                    if h is not None:
                        queries(h, 1)
                    high(4, f, XTF)
                    store(f)

            act.wait_ge(S("kt"), 1)
            A(kt0_h[:, :], kt0[:, :], ACT.Identity).then_inc(S("kt0_h"), 1)

            def split(n):
                half, at = next((k % 2, at) for k, load in enumerate(STAGED) for m, at in load if m == n)
                act.wait_ge(S("ld_" + n), 16)
                if n == "wc":
                    act.wait_ge(S("wc_sum"), 1)
                A(wh[n][:, :], stage[half][:, at:at + widths[n]], ACT.Identity).then_inc(S("split_h"), 1)

            split("wq")
            head(0)
            queries(0, 0)
            queries(0, 1)
            act.wait_ge(S("v1"), 1)
            A(v1_h[:, :], v1[:, :], ACT.Identity).then_inc(S("v1_ready"), 1)
            act.wait_ge(S("g_ps"), 1)
            A(g_h[:, :], I_(0)[:, 0:KC * P], ACT.Identity).then_inc(S("g_ready"), 1)
            act.wait_ge(S("gb_ps"), 1)
            A(gb[:, :], I_(1)[:, 0:P], ACT.Identity).then_inc(S("gb_ready"), 1)
            act.wait_ge(S("ld_late"), 16 * LATE)
            A(kva[3 * PW:SROWS, 0:PAIRS * P], ind[3 * PW:SROWS, :], ACT.Identity).then_inc(S("ind"), 1)
            for n in ("ga", "w1", "w2", "lb"):
                split(n)
            body(0, None, 1)
            for n in ("wi", "wo", "wc"):
                split(n)
            act.wait_ge(S("kvc_stored"), 16 * BATCH * 5)
            with act.Fori(1, NBLK - 1) as i:
                body(i, i - 1, i + 1)
            body(NBLK - 1, NBLK - 2, None)
            body(None, NBLK - 1, None)

        @block.vector
        def _(dve):
            V = nc.vector
            SUB, ADD, MULT, MAX = ALU.subtract, ALU.add, ALU.mult, ALU.max

            def norm_stats(j, b, src):
                st, mv, ve, nm = lnst[j][:4]
                for t in range(NT):
                    V.bn_stats(r3(st, NT)[:, t, :], src[:, t, :]).then_inc(S(f"ln{j}_st"), 1)
                even, odd, both = r3(st, NT)[:, :, 0:3], r3(st, NT)[:, :, 3:6], r3(mv, 3)
                dve.wait_ge(S(f"ln{j}_st"), (b + 1) * NT)
                V.tensor_tensor(both[:, 0, :], even[:, :, 1], odd[:, :, 1], ADD).then_inc(S(f"ln{j}_mv"), 1)
                V.tensor_tensor(both[:, 1, :], even[:, :, 1], odd[:, :, 1], SUB).then_inc(S(f"ln{j}_mv"), 1)
                V.tensor_tensor(both[:, 2, :], even[:, :, 2], odd[:, :, 2], ADD).then_inc(S(f"ln{j}_mv"), 1)
                dve.wait_ge(S(f"ln{j}_mv"), b * 5 + 3)
                V.tensor_scalar(nm[:, :], both[:, 0, :], -0.5, None, MULT).then_inc(S(f"ln{j}_ve"), 1)
                V.tensor_tensor(both[:, 1, :], both[:, 1, :], both[:, 1, :], MULT).then_inc(S(f"ln{j}_mv"), 1)
                V.tensor_scalar(both[:, 2, :], both[:, 2, :], 1.0 / D, EPS, MULT, ADD).then_inc(S(f"ln{j}_mv"), 1)
                dve.wait_ge(S(f"ln{j}_mv"), b * 5 + 5)
                V.scalar_tensor_tensor(out=ve[:, :], in0=both[:, 1, :], scalar=0.25, in1=both[:, 2, :],
                                       op0=MULT, op1=ADD).then_inc(S(f"ln{j}_ve"), 1)

            def low(j, b, dst):
                for c in range(KC):
                    dve.wait_ge(S(f"ln{j}_h"), b * KC + c + 1)
                    V.tensor_tensor(dst[1][:, c, :], T_(c), as32(dst[0][:, c, :]), SUB).then_inc(S(f"ln{j}_l"), 1)

            def queries_low(b, m):
                dve.wait_ge(S("qh"), b * KC + m + 1)
                V.scalar_tensor_tensor(out=QO[1][:, m, :], in0=S_(m), scalar=cols[:, BQ + m:BQ + m + 1],
                                       in1=as32(QO[0][:, m, :]), op0=ADD, op1=SUB).then_inc(S("ql"), 1)

            def row_max(b, t):
                dve.wait_ge(S("row_sc"), b * NT + t + 1)
                V.reduce_max(MX[:, t, :], psS[:, :].rearrange("p (h k) -> p h k", h=HEADS), AX.X).then_inc(S("mx"), 1)

            def reciprocal_sums(b, m, part):
                dve.wait_ge(S("pv"), b * PAIRS + (m + 1) * GPC)
                lo = part * T // 2
                V.reciprocal(rec[:, lo:lo + T // 2], T_(1)[:, lo:lo + T // 2]).then_inc(S("rec"), 1)

            def attended(b, m):
                dve.wait_ge(S("rec"), b * KC * 2 + 2 * m + 2)
                if m == 1:
                    dve.wait_ge(S("ol"), b * KC + 1)
                V.tensor_tensor(o32[:, :], T_(0), rec[:, :], MULT).then_inc(S("o32"), 1)

            def first_residual(b, half):
                dve.wait_ge(S("x1_ps"), b * 2 + half + 1)
                dve.wait_ge(S("xres"), b + 1)
                bank = (P0, I_(2))[half]
                V.tensor_tensor(xmid[:, half * 2 * D:(half + 1) * 2 * D], bank, xmid[:, half * 2 * D:(half + 1) * 2 * D],
                                ADD).then_inc(S("x1"), 1)

            def experts(b):
                lg3, srt3, idx3, idxf3 = (r3(t, NT) for t in (lg, srt, idx, idxf))
                for t in range(NT):
                    dve.wait_ge(S("ga_ps"), b * 2 + t // 2 + 1)
                    o = (t % 2) * 256 + EXPERTS * RANK
                    V.tensor_tensor(lg3[:, t, :], I_(t // 2)[:, o:o + EXPERTS], gbrow[:, :], ADD).then_inc(S("lg"), 1)
                dve.wait_ge(S("lg"), (b + 1) * NT)
                V.tensor_copy(gnum[:, :], lg3[:, :, 0])
                for t in range(NT):
                    V.max(srt3[:, t, :], lg3[:, t, :]).then_inc(S("srt"), 1)
                dve.wait_ge(S("srt"), (b + 1) * NT)
                V.tensor_tensor(r3(srtd, NT), srt3, srt3[:, :, 0:1].broadcast_to([P, NT, EXPERTS]), SUB).then_inc(
                    S("srtd"), 1)
                for t in range(NT):
                    V.max_index(idx3[:, t, :], srt3[:, t, :], lg3[:, t, :]).then_inc(S("idx"), 1)
                dve.wait_ge(S("idx"), (b + 1) * NT)
                V.tensor_copy(idxf[:, :], idx[:, :]).then_inc(S("idxf"), 1)
                dve.wait_ge(S("idxf"), b + 1)
                for q in range(2):
                    for t in range(NT):
                        o = (t % 2) * 256
                        V.scalar_tensor_tensor(out=r1[:, (2 * q) * T + t * P:(2 * q) * T + (t + 1) * P], in0=eid[:, :],
                                               scalar=idxf3[:, t, q:q + 1], in1=I_(t // 2)[:, o:o + P],
                                               op0=ALU.is_equal, op1=MULT).then_inc(S("masked"), 1)
                dve.wait_ge(S("masked"), (b + 1) * 2 * NT)
                V.tensor_tensor(r1[:, T:2 * T], r1[:, 2 * T:3 * T], r1[:, 0:T], SUB).then_inc(S("am"), 2)

            def gates(b):
                dve.wait_ge(S("srte"), b + 1)
                e3 = r3(srte, NT)
                V.reduce_sum(gsum[:, :], e3, AX.X).then_inc(S("gsum"), 1)
                V.tensor_tensor(gnum[:, :], e3[:, :, 0], e3[:, :, 1], ADD).then_inc(S("gsum"), 1)
                dve.wait_ge(S("gsum"), (b + 1) * 2)
                V.reciprocal(grec[:, :], gsum[:, :]).then_inc(S("grec"), 1)
                dve.wait_ge(S("grec"), b + 1)
                V.tensor_tensor(gate[:, :], gnum[:, :], grec[:, :], MULT).then_inc(S("gate"), 1)

            def lora_low(b):
                for q in range(2):
                    dve.wait_ge(S("ath"), b * 2 + q + 1)
                    V.tensor_tensor(AT[1][:, q, :], T_(q), as32(AT[0][:, q, :]), SUB).then_inc(S("atl"), 1)

            def hidden_sum(b, f):
                dve.wait_ge(S("second_ps"), b * NFF + f + 1)
                V.scalar_tensor_tensor(out=R1[:, f % 3, :], in0=I_(ibank(f)), scalar=nbi[:, f:f + 1],
                                       in1=R1[:, f % 3, :], op0=MAX, op1=ADD).then_inc(S("hid"), 1)

            def second_residual(b, half):
                dve.wait_ge(S("x2_ps"), b * 2 + half + 1)
                dve.wait_ge(S("stored"), (b + 1) * 16)
                dve.wait_ge(S("gate"), b + 1)
                cols2 = slice(half * 2 * D, (half + 1) * 2 * D)
                V.tensor_tensor(r3(xo, NT)[:, 2 * half:2 * half + 2, :], I_(half).rearrange("p (t n) -> p t n", t=2),
                                crow[:, :].unsqueeze(1).broadcast_to([P, 2, D]), ADD).then_inc(S("ymid"), 1)
                dve.wait_ge(S("ymid"), b * 2 + half + 1)
                for t in (2 * half, 2 * half + 1):
                    V.scalar_tensor_tensor(out=XO[:, t, :], in0=XO[:, t, :], scalar=gate[:, t:t + 1],
                                           in1=XMID[:, t, :], op0=MULT, op1=ADD).then_inc(S("x2"), 1)

            def weights_shift(b):
                dve.wait_ge(S("sc1_ps"), b + 1)
                V.tensor_tensor(SC1, S_(0)[:, 0:NT * KEYS].rearrange("p (t k) -> p t k", t=NT),
                                gbcur[:, :].unsqueeze(1).broadcast_to([P, NT, KEYS]), ADD).then_inc(S("sc1b"), 1)
                dve.wait_ge(S("sc1b"), b + 1)
                V.reduce_max(mx1[:, :], SC1, AX.X).then_inc(S("mx1"), 1)
                dve.wait_ge(S("mx1"), b + 1)
                V.tensor_tensor(SC1, SC1, mx1[:, :].unsqueeze(2).broadcast_to([P, NT, KEYS]), SUB).then_inc(
                    S("sc1"), 1)

            def weights_sums(b):
                dve.wait_ge(S("ex1"), b + 1)
                V.reduce_sum(sum1[:, :], SC1, AX.X).then_inc(S("sum1"), 1)
                dve.wait_ge(S("sum1"), b + 1)
                V.reciprocal(rec1[:, :], sum1[:, :]).then_inc(S("rec1"), 1)

            def weights_low(b):
                dve.wait_ge(S("eh"), b + 1)
                V.tensor_tensor(AT[1][:, 0, 0:2 * P], S_(1)[:, 0:2 * P], as32(AT[0][:, 0, 0:2 * P]), SUB).then_inc(
                    S("el"), 1)

            def third_residual(b, odd):
                dve.wait_ge(S("p1"), b * 2 + odd + 1)
                dve.wait_ge(S("rec1"), b + 1)
                for u in range(NT // 2):
                    t = 2 * u + odd
                    V.scalar_tensor_tensor(out=XO[:, t, :], in0=I_(odd)[:, u * D:(u + 1) * D], scalar=rec1[:, t:t + 1],
                                           in1=XO[:, t, :], op0=MULT, op1=ADD).then_inc(S("x3"), 1)

            def fourth_residual(b, half):
                dve.wait_ge(S("x4_ps"), b * 2 + half + 1)
                for t in (2 * half, 2 * half + 1):
                    o = (t % 2) * D
                    V.tensor_tensor(XO[:, t, :], I_(half)[:, o:o + D], XO[:, t, :], ADD).then_inc(S("x4"), 1)

            def body(a, f, h):
                if f is not None:
                    dve.wait_ge(S("x1"), (f + 1) * 2)
                    norm_stats(2, f, XMID)
                if a is not None:
                    row_max(a, 0)
                if f is not None:
                    low(2, f, XTF)
                if a is not None:
                    row_max(a, 1)
                    row_max(a, 2)
                if f is not None:
                    experts(f)
                if a is not None:
                    row_max(a, 3)
                if f is not None:
                    gates(f)
                    lora_low(f)
                for s in range(NFF):
                    if f is not None:
                        hidden_sum(f, s)
                    if a is not None:
                        for m, part, slot in ((0, 0, 2), (0, 1, 3), (1, 0, 4), (1, 1, 5)):
                            if s == slot:
                                reciprocal_sums(a, m, part)
                                if part:
                                    attended(a, m)
                if f is not None:
                    second_residual(f, 0)
                    second_residual(f, 1)
                    dve.wait_ge(S("x2"), (f + 1) * NT)
                    norm_stats(3, f, XO)
                if a is not None:
                    first_residual(a, 0)
                if f is not None:
                    low(3, f, XTF)
                if a is not None:
                    first_residual(a, 1)
                if h is not None:
                    dve.wait_ge(S("x_in"), (h + 1) * 16)
                    norm_stats(1, h, XIN)
                if f is not None:
                    weights_shift(f)
                if h is not None:
                    low(1, h, XTA)
                if f is not None:
                    weights_sums(f)
                    weights_low(f)
                if h is not None:
                    queries_low(h, 0)
                if f is not None:
                    third_residual(f, 0)
                    third_residual(f, 1)
                    dve.wait_ge(S("x3"), (f + 1) * NT)
                    norm_stats(4, f, XO)
                if h is not None:
                    queries_low(h, 1)
                if f is not None:
                    low(4, f, XTF)
                    fourth_residual(f, 0)
                    fourth_residual(f, 1)

            V.memset(mhalf[:, :], -0.5).then_inc(S("mhalf"), 1)
            dve.wait_ge(S("ld_small"), 16 * 8)
            V.tensor_scalar(nbi[:, :], cols[:, BI:BI + NFF], -1.0, None, MULT).then_inc(S("nbi"), 1)
            for n, (kt, col) in enumerate(((kt0, BK0), (kt1, BK1))):
                dve.wait_ge(S("kt_ps"), n + 1)
                ktv = r3(kt, KC)
                V.tensor_tensor(ktv, I_(n)[:, 0:KC * P].rearrange("p (m n) -> p m n", m=KC),
                                cols[:, col:col + KC].unsqueeze(2).broadcast_to([P, KC, P]), ADD).then_inc(S("kt"), 1)
            dve.wait_ge(S("x_in"), 16)
            norm_stats(1, 0, XIN)
            dve.wait_ge(S("kt0_h"), 1)
            V.tensor_tensor(kt0_l[:, :], kt0[:, :], as32(kt0_h[:, :]), SUB).then_inc(S("kt0_l"), 1)
            for hl, kt in enumerate((kt0_h, kt0_l)):
                if hl:
                    dve.wait_ge(S("kt0_l"), 1)
                for b in range(BATCH):
                    for m in range(KC):
                        V.tensor_tensor(
                            KB[hl][:, b * KC + m, :].rearrange("p (h k) -> p h k", h=8),
                            as32(kt[:, m * P + b * KEYS:m * P + (b + 1) * KEYS]).unsqueeze(1).broadcast_to([P, 8, KEYS]),
                            kmask[:, :].unsqueeze(2).broadcast_to([P, 8, KEYS]), MULT).then_inc(S("kb_split"), 1)
            dve.wait_ge(S("v0_ps"), 1)
            V.tensor_tensor(r3(v0, BATCH), I_(2).rearrange("p (b n) -> p b n", b=BATCH),
                            bvrow0[:, :].unsqueeze(1).broadcast_to([P, BATCH, D]), ADD).then_inc(S("v0"), 1)
            dve.wait_ge(S("v1_ps"), 1)
            V.tensor_tensor(r3(v1, BATCH), P0.rearrange("p (b n) -> p b n", b=BATCH),
                            bvrow1[:, :].unsqueeze(1).broadcast_to([P, BATCH, D]), ADD).then_inc(S("v1"), 1)
            dve.wait_ge(S("v0"), 1)
            V.tensor_tensor(r3(v0, BATCH), r3(v0, BATCH), vmask[:, :].unsqueeze(1).broadcast_to([P, BATCH, D]),
                            MULT).then_inc(S("v0_ready"), BATCH)

            def split(n):
                half, at = next((k % 2, at) for k, load in enumerate(STAGED) for m, at in load if m == n)
                dve.wait_ge(S("split_h"), SPLIT_ORDER.index(n) + 1)
                V.tensor_tensor(wl[n][:, :], stage[half][:, at:at + widths[n]], as32(wh[n][:, :]), SUB).then_inc(
                    S("split_l"), 1)

            split("wq")
            low(1, 0, XTA)
            queries_low(0, 0)
            queries_low(0, 1)
            dve.wait_ge(S("v1_ready"), 1)
            V.tensor_tensor(v1_l[:, :], v1[:, :], as32(v1_h[:, :]), SUB).then_inc(S("v1_ready"), 1)
            dve.wait_ge(S("g_ready"), 1)
            V.tensor_tensor(g_l[:, :], I_(0)[:, 0:KC * P], as32(g_h[:, :]), SUB).then_inc(S("g_ready"), 1)
            for n in ("ga", "w1", "w2", "lb"):
                split(n)
            body(0, None, 1)
            split("wi")
            dve.wait_ge(S("stored"), 16)
            dve.wait_ge(S("crow_ps"), 1)
            V.scalar_tensor_tensor(out=crow[:, :], in0=borow[:, :], scalar=2.0, in1=I_(1)[:, 0:D],
                                   op0=MULT, op1=ADD).then_inc(S("crow"), 1)
            split("wo")
            dve.wait_ge(S("ld_wc"), 16)
            dve.wait_ge(S("ld_late"), 16 * LATE)
            V.tensor_tensor(r3(stage[0], KC, 0, KC * D), r3(stage[0], KC, 0, KC * D),
                            disha[:, :].unsqueeze(1).broadcast_to([P, KC, D]), ADD).then_inc(S("wc_sum"), 1)
            split("wc")
            dve.wait_ge(S("nbi"), 1)
            with dve.Fori(1, NBLK - 1) as i:
                body(i, i - 1, i + 1)
            body(NBLK - 1, NBLK - 2, None)
            body(None, NBLK - 1, None)

        @block.gpsimd
        def _(pool):
            G_ = nc.gpsimd

            def scale(j, b):
                _, _, ve, nm, rs, nmr = lnst[j]
                pool.wait_ge(S(f"ln{j}_ve"), (b + 1) * 2)
                G_.tensor_tensor(rs[:, :], ve[:, :], mhalf[:, :], ALU.pow).then_inc(S(f"ln{j}_rs"), 1)
                pool.wait_ge(S(f"ln{j}_rs"), b + 1)
                G_.tensor_tensor(nmr[:, :], nm[:, :], rs[:, :], ALU.mult).then_inc(S(f"ln{j}_nmr"), 1)

            def attended_low(b, m):
                pool.wait_ge(S("oh"), b * KC + m + 1)
                G_.tensor_tensor(QO[1][:, m, :], o32[:, :], as32(QO[0][:, m, :]), ALU.subtract).then_inc(S("ol"), 1)

            def hidden_low(b, f):
                pool.wait_ge(S("hsh"), b * NF1 + f + 1)
                G_.tensor_tensor(HS[1][:, f, :], HS32[:, f % 2, :], as32(HS[0][:, f, :]), ALU.subtract).then_inc(
                    S("hsl"), 1)

            def sum_low(b, f):
                pool.wait_ge(S("hidh"), b * NFF + f + 1)
                G_.tensor_tensor(HL[:, f, :], R1[:, f % 3, :], as32(HH[:, f, :]), ALU.subtract).then_inc(S("hidl"), 1)

            def residual(a, f):
                if f is not None:
                    pool.wait_ge(S("x2"), (f + 1) * NT)
                pool.wait_ge(S("x_in"), (a + 1) * 16)
                G_.tensor_tensor(XMID, XIN, b2row[:, :].unsqueeze(1).broadcast_to([P, NT, D]), ALU.add).then_inc(
                    S("xres"), 1)

            def body(a, f, h):
                if f is not None:
                    scale(2, f)
                for s in range(NFF):
                    if f is not None and s >= 1:
                        sum_low(f, s - 1)
                    if a is not None and s in (5, 6):
                        attended_low(a, s - 5)
                if f is not None:
                    sum_low(f, NFF - 1)
                if a is not None:
                    if f is None:
                        residual(a, f)
                    for c in range(NF1):
                        hidden_low(a, c)
                if f is not None:
                    scale(3, f)
                if a is not None and f is not None:
                    residual(a, f)
                if h is not None:
                    scale(1, h)
                if f is not None:
                    scale(4, f)

            pool.wait_ge(S("mhalf"), 1)
            scale(1, 0)
            pool.wait_ge(S("ld_late"), 16 * LATE)
            body(0, None, 1)
            with pool.Fori(1, NBLK - 1) as i:
                body(i, i - 1, i + 1)
            body(NBLK - 1, NBLK - 2, None)
            body(None, NBLK - 1, None)


IN = ["x", "wk0", "wv0", "wk1", "wv1", "wq1t", "ctx", "ctxd", "cols", "kmask", "ident", "vmask", "bvrow0", "bvrow1",
      "eid", "ones_pair", "b2row", "gbrow", "disha", "borow", "ind", "wq", "ga", "w1", "w2", "lb", "wi", "wo", "wc"]


def kernel(x, ctx_768, **w):
    import concourse.bacc as bacc
    from concourse.bass_utils import run_bass_kernel_spmd

    def rows(a):
        a = np.asarray(a)
        return a.reshape(-1, P, a.shape[1]).transpose(1, 0, 2).reshape(P, -1)

    def crows(a):
        a = np.asarray(a)
        return a.reshape(2, CK, a.shape[1]).transpose(1, 0, 2).reshape(CK, -1)

    def col(v):
        return np.asarray(v).reshape(-1, P).T

    def every(v):
        return np.broadcast_to(np.asarray(v)[None, :], (P, v.shape[0]))

    def masks():
        p = np.arange(P)
        c = np.arange(D)
        key = np.arange(PAIRS * P)
        ind = np.zeros((HEADS, PAIRS * P), np.float32)
        ind[2 * (key // P) + (key % P) // KEYS, key] = -1.0
        return {
            "kmask": (p[:, None] // HD == np.arange(8)[None, :]).astype(np.float32),
            "ident": np.eye(P, dtype=np.float32),
            "vmask": (p[:, None] // KEYS == (c[None, :] // HD) % 2).astype(np.float32),
            "ones_pair": (p[:, None] // KEYS == np.arange(PW)[None, :] // HD).astype(np.float32),
            "eid": np.broadcast_to((p // RANK).astype(np.float32)[None, :], (P, P)),
            "ind": ind,
        }

    ct = np.asarray(ctx_768).reshape(BATCH * KEYS, DC).T.reshape(2, CK, BATCH, KEYS).transpose(1, 0, 2, 3)
    arrays = {
        "x": np.asarray(x).reshape(BATCH * SEQ, D),
        "ctx": ct.reshape(CK, -1),
        "ctxd": np.concatenate([ct, ct], axis=3).reshape(CK, -1),
        "wk0": crows(w["L0_xattn_Wk"]), "wv0": crows(w["L0_xattn_Wv"]),
        "wk1": crows(w["L1_xattn_Wk"]), "wv1": crows(w["L1_xattn_Wv"]),
        "wq1t": rows(np.asarray(w["L1_xattn_Wq"]).T),
        "cols": np.concatenate([col(w[n]) for n in ("L0_xattn_bq", "L0_xattn_b1", "L0_ffn_bi", "L0_xattn_bk",
                                                    "L1_xattn_bk", "L1_xattn_bq")], axis=1),
        "bvrow0": every(w["L0_xattn_bv"]), "bvrow1": every(w["L1_xattn_bv"]),
        "b2row": every(w["L0_xattn_b2"]), "gbrow": every(w["L0_ffn_gate_b"]), "borow": every(w["L0_ffn_bo"]),
        "disha": np.concatenate([np.asarray(w["L1_ffn_disha"])] * 2, axis=0),
        "wq": rows(w["L0_xattn_Wq"]), "w1": rows(w["L0_xattn_W1"]), "w2": rows(w["L0_xattn_W2"]),
        "ga": rows(np.concatenate([np.asarray(w["L0_ffn_lora_A"]).reshape(EXPERTS * RANK, D),
                                   np.asarray(w["L0_ffn_gate_w"])], axis=0).T),
        "lb": np.asarray(w["L0_ffn_lora_B"]).transpose(0, 2, 1).reshape(EXPERTS * RANK, DFF),
        "wi": rows(np.asarray(w["L0_ffn_wi"]).T), "wo": rows(np.asarray(w["L0_ffn_wo"]).T),
        "wc": rows(np.asarray(w["L1_ffn_weight"]).T),
        **masks(),
    }
    nc = bacc.Bacc("TRN2", target_bir_lowering=False, num_devices=1)
    io, feeds = {}, {}
    for n in IN:
        feeds[f"in_{n}"] = np.ascontiguousarray(arrays[n])
        io[n] = nc.dram_tensor(f"in_{n}", feeds[f"in_{n}"].shape, F32, kind="ExternalInput").ap()
    io["out"] = nc.dram_tensor("out", (BATCH * SEQ, D), F32, kind="ExternalOutput").ap()
    build(nc, io)
    r = run_bass_kernel_spmd(nc, [feeds], core_ids=[0])
    return r.results[0]["out"].reshape(BATCH, SEQ, D)
```

```python
import numpy as np
import concourse.bass as bass
import concourse.mybir as mybir

F32 = mybir.dt.float32
F32R = mybir.dt.float32r
U32 = mybir.dt.uint32
ALU = mybir.AluOpType
ACT = mybir.ActivationFunctionType
AX = mybir.AxisListType

P = 128
BATCH, SEQ, D = 2, 1024, 256
KEYS, DC = 64, 192
HEADS = 16
HD = D // HEADS
F1 = 512
DFF, EXPERTS, RANK = 1024, 8, 16
T = 256
NT = T // P
NBLK = BATCH * SEQ // T
BPB = SEQ // T
KC = D // P
PAIRS = HEADS // 2
PW = 2 * HD
GPC = P // PW
CK = DC // 2
NF1 = F1 // P
NFF = DFF // P
GA = EXPERTS * RANK + EXPERTS
SROWS = 3 * PW + HEADS
EPS = 1e-5
SCALE = float(HD) ** -0.5

DPAIRS = PAIRS // 2
NDF = NFF // 2
NDH = NF1 // 2

KV_S = PAIRS * P
HPC = HEADS // KC
KV_B = KC * HPC * KEYS
KV_C = 2 * KC * KEYS + 2 * D

WIDTHS = {"wq": KC * D, "ga": KC * GA, "w1": KC * F1, "w2": NF1 * D, "lb": DFF, "wi": KC * DFF, "wo": NFF * D,
          "wc": KC * D}
CHUNKS = {"wq": KC, "ga": KC, "w1": KC, "w2": NF1, "lb": 1, "wi": KC, "wo": NFF, "wc": KC}
SPLIT_ORDER = ["wq", "w1", "w2", "ga", "wi", "lb", "wo", "wc"]
SPARE = 2560

KEPT = [("ident", P), ("cols", 20), ("kmask", 8), ("ones_pair", PW), ("b2row", D), ("gbrow", EXPERTS), ("eid", P)]
PASSING = [("vmask", D), ("bvrow0", D), ("bvrow1", D), ("wq1t", KC * D)]
BQ, B1, BI, BK0, BK1, BQ1 = 0, 2, 6, 14, 16, 18


def build(nc, io):
    sb = lambda name, shape, dt=F32: nc.alloc_sbuf_tensor(name, [shape[0], int(np.prod(shape[1:]))], dt)
    sems = {}

    def sem(name):
        if name not in sems:
            sems[name] = nc.alloc_semaphore(name)
        return sems[name]

    def r3(t, a, lo=0, hi=None, rows=P):
        v = t[0:rows, lo:hi] if hi is not None else t[0:rows, lo:]
        return v.rearrange("p (a n) -> p a n", a=a)

    def pair(name, a, width):
        return tuple(r3(sb(f"{name}_{hl}", [P, width], F32R), a) for hl in "hl")

    room = nc.sbuf_base
    hid_h, hid_l = sb("hid_h", [P, NFF * T], F32R), sb("hid_l", [P, NFF * T], F32R)
    HH, HL = r3(hid_h, NFF), r3(hid_l, NFF)
    r1 = sb("r1", [P, NFF * T])
    R1 = r3(r1, NFF)
    XTC = pair("xtc", KC, KC * T)
    XTD = pair("xtd", KC, KC * T)
    AT = pair("at", 2, 2 * T)
    ET = pair("et", 1, P)
    x2, x3, x4 = (sb(n, [P, NT * D]) for n in ("x2", "x3", "x4"))
    X2, X3, X4 = (r3(t, NT) for t in (x2, x3, x4))
    xn3, xn4 = (sb(n, [P, NT * D]) for n in ("xn3", "xn4"))
    spare = sb("spare", [P, SPARE])
    room2 = -(-nc.sbuf_base // 32) * 32
    XTF = pair("xtf", KC, KC * T)
    am = sb("am", [P, 3 * T])
    xn2 = sb("xn2", [P, NT * D])
    room_end = nc.sbuf_base

    wh = {n: sb(n + "_h", [P, w], F32R) for n, w in WIDTHS.items()}
    wl = {n: sb(n + "_l", [P, w], F32R) for n, w in WIDTHS.items()}
    WH = {n: r3(wh[n], CHUNKS[n]) for n in WIDTHS}
    WL = {n: r3(wl[n], CHUNKS[n]) for n in WIDTHS}

    def views(t, parts):
        out, at = {}, 0
        for n, width in parts:
            out[n] = t[:, at:at + width]
            at += width
        return out

    kept = sb("kept", [P, sum(n for _, n in KEPT)])
    k_ = views(kept, KEPT)
    ident, cols, kmask, ones_pair, b2row, gbrow, eid = (k_[n] for n, _ in KEPT)
    nbi = sb("nbi", [P, NFF])
    crow = sb("crow", [P, D])
    mhalf = sb("mhalf", [P, NT])

    xin, xr, xmid, xg, xn1 = (sb(n, [P, NT * D]) for n in ("xin", "xr", "xmid", "xg", "xn1"))
    XIN, XMID, XG = r3(xin, NT), r3(xmid, NT), r3(xg, NT)
    XN = {j: r3(t, NT) for j, t in ((1, xn1), (2, xn2), (3, xn3), (4, xn4))}
    XTA = pair("xta", KC, KC * T)
    QU = pair("qu", KC, KC * T)
    OA = pair("oa", KC, KC * T)
    HS = pair("hs", NF1, NF1 * T)
    hs32 = sb("hs32", [P, NF1 * T])
    HS32 = r3(hs32, NF1)
    stack = sb("stack", [SROWS, PAIRS * T], F32R)
    QS = r3(stack, PAIRS, rows=SROWS)
    mx = sb("mx", [P, NT * HEADS])
    MX = r3(mx, NT)
    mxT = sb("mxT", [HEADS, T], F32R)
    ks = sb("ks", [SROWS, KV_S], F32R)
    KS = r3(ks, PAIRS, rows=SROWS)
    kbh = sb("kbh", [P, KV_B], F32R)
    KBH = r3(kbh, KC)
    vcur = sb("vcur", [P, D])
    kvc = sb("kvc", [P, KV_C], F32R)
    G = (r3(kvc, KC, 0, KC * KEYS), r3(kvc, KC, KC * KEYS, 2 * KC * KEYS))
    V1 = (kvc[:, 2 * KC * KEYS:2 * KC * KEYS + D], kvc[:, 2 * KC * KEYS + D:KV_C])
    gbcur = sb("gbcur", [P, KEYS])
    ex = sb("ex", [P, PAIRS * T])
    EX = r3(ex, PAIRS)
    rec, o32 = sb("rec", [P, KC * T]), sb("o32", [P, KC * T])
    REC, O32 = r3(rec, KC), r3(o32, KC)
    lnst = {j: (sb(f"st{j}", [P, NT * 6]), sb(f"mv{j}", [P, NT * 3]), sb(f"ve{j}", [P, NT]), sb(f"nm{j}", [P, NT]),
                sb(f"rs{j}", [P, NT]), sb(f"nmr{j}", [P, NT])) for j in (1, 2, 3, 4)}
    lg, srt, srtd, srte = (sb(n, [P, NT * EXPERTS]) for n in ("lg", "srt", "srtd", "srte"))
    idx = sb("idx", [P, NT * EXPERTS], U32)
    idxf = sb("idxf", [P, NT * EXPERTS])
    gsum, grec, gnum, gate = (sb(n, [P, NT]) for n in ("gsum", "grec", "gnum", "gate"))
    sc1 = sb("sc1", [P, NT * KEYS])
    SC1 = r3(sc1, NT)
    mx1, sum1, rec1 = (sb(n, [P, NT]) for n in ("mx1", "sum1", "rec1"))

    place = [-(-room // 32) * 32]

    def temp(name, shape, dt=F32):
        n = int(np.prod(shape[1:]))
        t = nc.alloc_sbuf_tensor_at(name, [shape[0], n], dt, offset=place[0])
        place[0] += 4 * n
        assert place[0] <= room_end, (name, place[0] - room_end)
        return t

    at0 = place[0]
    kvw = temp("kvw", [CK, 3 * 2 * D + 2 * BATCH * 2 * KEYS])
    a1 = temp("a1", [CK, 2 * D + 2 * BATCH * KEYS])
    at1 = place[0]
    kb_h, kb_l = temp("kb_h", [P, BATCH * KC * 512], F32R), temp("kb_l", [P, BATCH * KC * 512], F32R)
    KB = (r3(kb_h, BATCH * KC), r3(kb_l, BATCH * KC))
    STG = {n: temp("stage_" + n, [P, WIDTHS[n]]) for n in ("wq", "w1", "w2", "ga", "lb")}
    STG["wi"] = nc.alloc_sbuf_tensor_at("stage_wi", [P, WIDTHS["wi"]], F32, offset=at0)
    STG["wo"] = nc.alloc_sbuf_tensor_at("stage_wo", [P, WIDTHS["wo"]], F32, offset=at1)
    v1, v1_h, v1_l = (temp(n, [P, BATCH * D], dt) for n, dt in (("v1", F32), ("v1_h", F32R), ("v1_l", F32R)))
    g_h, g_l = temp("g_h", [P, KC * P], F32R), temp("g_l", [P, KC * P], F32R)
    v0 = temp("v0", [P, BATCH * D])
    gb = temp("gb", [P, BATCH * KEYS])
    late = temp("late", [P, 2 * D])
    STG["wc"] = temp("stage_wc", [P, WIDTHS["wc"]])
    ind = ex
    assert place[0] <= room2, place[0] - room2
    place[0] = room2
    passing = temp("passing", [P, sum(n for _, n in PASSING)])
    p_ = views(passing, PASSING)
    vmask, bvrow0, bvrow1, wq1t = (p_[n] for n, _ in PASSING)
    kt0, kt1 = temp("kt0", [P, KC * P]), temp("kt1", [P, KC * P])
    kt0_h, kt0_l = temp("kt0_h", [P, KC * P], F32R), temp("kt0_l", [P, KC * P], F32R)
    WV0, WK1, WV1, CTXD = 0, 2 * D, 4 * D, 6 * D
    CTX = 2 * D

    dr = lambda n, shape: nc.dram_tensor(n, shape, F32, kind="Internal").ap()
    dr_ks, dr_kb = dr("dr_ks", (3 * PW, BATCH * KV_S)), dr("dr_kb", (P, BATCH * KV_B))
    dr_v, dr_gb = dr("dr_v", (P, BATCH * D)), dr("dr_gb", (P, BATCH * KEYS))
    dr_c = dr("dr_c", (P, BATCH * KV_C))

    psT, psI, psS, psP = (nc.alloc_psum_tensor(n, [P, 1024], F32) for n in ("psT", "psI", "psS", "psP"))
    T_, I_, S_, P_ = (lambda k, t=t: t[:, 512 * k:512 * k + 512] for t in (psT, psI, psS, psP))

    as32 = lambda ap: ap.bitcast(F32)
    x_v = io["x"].rearrange("(b p t) d -> b p t d", p=P, t=NT)
    out_v = io["out"].rearrange("(b p t) d -> b p t d", p=P, t=NT)
    S = sem
    block = nc.Block()
    is0 = lambda b: isinstance(b, int) and b == 0

    with block:
        @block.sync
        def _(sp):
            def load_weight(n):
                sp.dma_start(STG[n][:, :], io[n]).then_inc(S("ld_" + n), 16)

            sp.dma_start(a1[:, :], io["a1"]).then_inc(S("ld_a1"), 16)
            sp.dma_start(kept[:, :], io["kept"]).then_inc(S("ld_kept"), 16)
            sp.dma_start(XIN, x_v[0]).then_inc(S("x_in"), 16)
            load_weight("wq")
            sp.dma_start(kvw[:, :], io["kvw"]).then_inc(S("ld_kvw"), 16)
            sp.dma_start(passing[:, :], io["passing"]).then_inc(S("ld_passing"), 16)
            sp.dma_start(ind[3 * PW:SROWS, 0:KV_S], io["ind"]).then_inc(S("ld_ind"), 16)
            load_weight("w1")
            load_weight("w2")

            def load_kb(b):
                if not is0(b):
                    sp.wait_ge(S("row_sc"), b * NT)
                sp.dma_start(as32(kbh[:, :]), dr_kb[:, bass.ds(b // BPB * KV_B, KV_B)]).then_inc(S("kbh"), 16)

            sp.wait_ge(S("kb_high"), KC)
            sp.dma_start(dr_kb, as32(kb_h[:, :])).then_inc(S("kb_stored"), 16)
            for r, half in ((0, kb_h), (1, kb_h), (2, kb_l)):
                if r == 2:
                    sp.wait_ge(S("kb_stored"), 16)
                    load_kb(0)
                    sp.wait_ge(S("kb_low"), KC)
                for g in range(GPC):
                    sp.dma_start(dr_ks[PW * r:PW * r + PW, :].rearrange("p (m g n) -> p m g n", g=GPC, n=P)[:, :, g, :],
                                 as32(r3(half, BATCH * KC)[PW * g:PW * g + PW, :, g * P:(g + 1) * P])).then_inc(
                        S("kv_stored"), 16)

            def load_keys(b):
                bb = b // BPB
                if not is0(b):
                    sp.wait_ge(S("pv"), b * KC)
                sp.dma_start(as32(ks[0:3 * PW, :]), dr_ks[:, bass.ds(bb * KV_S, KV_S)]).then_inc(S("ks"), 16)

            def load_v(b):
                sp.dma_start(vcur[:, :], dr_v[:, bass.ds(b // BPB * D, D)]).then_inc(S("vcur"), 16)

            def load_c(b):
                if not is0(b):
                    sp.wait_ge(S("p1"), b)
                bb = b // BPB
                sp.dma_start(as32(kvc[:, :]), dr_c[:, bass.ds(bb * KV_C, KV_C)]).then_inc(S("kvc"), 16)
                sp.dma_start(gbcur[:, :], dr_gb[:, bass.ds(bb * KEYS, KEYS)]).then_inc(S("kvc"), 16)

            def load_x(b):
                sp.wait_ge(S("ln1_xh"), b * NT)
                sp.wait_ge(S("xres"), b)
                sp.dma_start(XIN, x_v[b]).then_inc(S("x_in"), 16)

            def stack_q(b):
                sp.wait_ge(S("qh"), (b + 1) * KC)
                for r, half in ((0, 0), (2, 0), (1, 1)):
                    if r == 1:
                        sp.wait_ge(S("ql"), (b + 1) * KC)
                    for g in range(GPC):
                        dst = stack[PW * r:PW * r + PW, :].rearrange("p (m g n) -> p m g n", m=KC, g=GPC)[:, :, g, :]
                        sp.dma_start(as32(dst), as32(QU[half][PW * g:PW * g + PW, :, :])).then_inc(S("qstack"), 16)

            def stack_m(b):
                sp.wait_ge(S("mxT"), b + 1)
                sp.dma_start(as32(r3(stack, PAIRS, rows=SROWS)[3 * PW:SROWS, :, :]),
                             as32(mxT[:, :]).unsqueeze(1).broadcast_to([HEADS, PAIRS, T])).then_inc(S("mstack"), 16)

            def body(a, f, c, h):
                if h is not None:
                    if not is0(a):
                        load_x(h)
                    load_kb(h)
                if f is not None:
                    load_c(f)
                if h is not None:
                    load_keys(h)
                    load_v(h)
                    stack_q(h)
                    stack_m(h)

            load_x(1)
            load_weight("ga")
            sp.wait_ge(S("kv_stored"), 16 * 3 * GPC)
            load_keys(0)
            stack_q(0)
            sp.wait_ge(S("v0_ready"), 1)
            sp.dma_start(dr_v, v0[:, :]).then_inc(S("v_stored"), 16)
            stack_m(0)
            sp.wait_ge(S("v_stored"), 16)
            load_v(0)
            sp.wait_ge(S("proj"), 4)
            load_weight("wi")
            load_weight("lb")
            sp.dma_start(late[:, :], io["late"]).then_inc(S("stored"), 16)
            load_weight("wo")
            load_weight("wc")
            sp.wait_ge(S("g_ready"), 2)
            sp.wait_ge(S("v1_ready"), 2)
            sp.wait_ge(S("gb_ready"), 1)
            for hl, (gt, vt) in enumerate(((g_h, v1_h), (g_l, v1_l))):
                for b in range(BATCH):
                    o = b * KV_C + hl * KC * KEYS
                    sp.dma_start(dr_c[:, o:o + KC * KEYS].rearrange("p (m n) -> p m n", m=KC),
                                 as32(gt[:, :]).rearrange("p (m b n) -> p m b n", m=KC, b=BATCH)[:, :, b, :]).then_inc(
                        S("kvc_stored"), 16)
                o = 2 * KC * KEYS + hl * D
                sp.dma_start(dr_c.rearrange("p (b n) -> p b n", b=BATCH)[:, :, o:o + D],
                             as32(r3(vt, BATCH))).then_inc(S("kvc_stored"), 16)
            sp.dma_start(dr_gb, gb[:, :]).then_inc(S("kvc_stored"), 16)
            body(0, None, None, 1)
            sp.wait_ge(S("kvc_stored"), 16 * 7)
            body(1, 0, None, 2)
            with sp.Fori(2, NBLK - 1) as i:
                body(i, i - 1, i - 2, i + 1)
            body(NBLK - 1, NBLK - 2, NBLK - 3, None)
            body(None, NBLK - 1, NBLK - 2, None)
            sp.wait_ge(S("stored"), 16 * (NBLK + 1))

        @block.tensor
        def _(pe):
            mm = nc.tensor.matmul

            def three(out, lhs, rhs, chunks, passes=range(3), start=True, stop=True, **kw):
                n = len(chunks)
                for q in passes:
                    a, b = ((0, 0), (1, 0), (0, 1))[q]
                    for k, c in enumerate(chunks):
                        last = mm(out, lhs(a, c), rhs(b, c), start=start and q == 0 and k == 0,
                                  stop=stop and q == 2 and k == n - 1, **kw)
                return last

            def w(name, m, n=P):
                return lambda a, c: (WH, WL)[a][name][:, c, m:m + n]

            def x_of(halves, lo=0, n=T):
                return lambda a, c: halves[a][:, c, lo:lo + n]

            def transposes(j, b, bank):
                for t in range(NT):
                    pe.wait_ge(S(f"ln{j}_xh"), b * NT + t + 1)
                    for c in range(KC):
                        last = nc.tensor.transpose(bank[:, c * T + t * P:c * T + (t + 1) * P],
                                                   XN[j][:, t, c * P:(c + 1) * P], ident)
                last.then_inc(S(f"ln{j}_T"), 1)

            def split_in(j, b):
                pe.wait_ge(S(f"ln{j}_h"), b + 1)
                pe.wait_ge(S(f"ln{j}_l"), b + 1)

            def a_queries(b):
                split_in(1, b)
                if not is0(b):
                    pe.wait_ge(S("o32"), (b - 1) * KC + 1)
                for m in range(KC):
                    last = three(P_(0)[:, m * T:(m + 1) * T], w("wq", m * P), x_of(XTA), range(KC))
                last.then_inc(S("q_ps"), 1)

            def a_row_scores(b, t):
                if t == 0:
                    pe.wait_ge(S("kbh"), (b + 1) * 16)
                    pe.wait_ge(S("qh"), (b + 1) * KC)
                    if not is0(b):
                        pe.wait_ge(S("hs"), b * NDH)
                else:
                    pe.wait_ge(S("mx"), b * NT + t)
                for m in range(KC):
                    last = mm(S_(m), QU[0][:, m, t * P:(t + 1) * P], KBH[:, m, :], start=True, stop=True)
                last.then_inc(S("row_sc"), 1)

            def a_max_transposes(b):
                pe.wait_ge(S("mx"), (b + 1) * NT)
                if not is0(b):
                    pe.wait_ge(S("x1"), b)
                for t in range(NT):
                    last = nc.tensor.transpose(P_(1)[0:HEADS, t * P:(t + 1) * P], MX[:, t, :], ident)
                last.then_inc(S("mxT_ps"), 1)

            def a_scores(b, d):
                if d == 0:
                    pe.wait_ge(S("ks"), (b + 1) * 16)
                    pe.wait_ge(S("qstack"), (b + 1) * 16 * 3 * GPC)
                    pe.wait_ge(S("mstack"), (b + 1) * 16)
                if d >= 2:
                    pe.wait_ge(S("ex"), b * DPAIRS + d - 1)
                for k in range(2):
                    last = mm(S_(d % 2)[:, k * T:(k + 1) * T], KS[:, 2 * d + k, :], QS[:, 2 * d + k, :],
                              start=True, stop=True)
                last.then_inc(S("sc"), 1)

            def a_attend(b, m):
                if m == 0:
                    pe.wait_ge(S("vcur"), (b + 1) * 16)
                for d in (2 * m, 2 * m + 1):
                    pe.wait_ge(S("ex"), b * DPAIRS + d + 1)
                    for c in (2 * d, 2 * d + 1):
                        rows = slice(PW * (c % GPC), PW * (c % GPC) + PW)
                        mm(P_(m)[rows, 0:T], vcur[:, c * PW:(c + 1) * PW], EX[:, c, :], start=True, stop=True)
                        last = mm(P_(m)[rows, T:2 * T], ones_pair, EX[:, c, :], start=True, stop=True)
                last.then_inc(S("pv"), 1)

            def a_hidden(b, u):
                if u == 0:
                    pe.wait_ge(S("oh"), (b + 1) * KC)
                    pe.wait_ge(S("ol"), (b + 1) * KC)
                for k in range(2):
                    last = three(S_(u)[:, k * T:(k + 1) * T], w("w1", (2 * u + k) * P), x_of(OA), range(KC))
                last.then_inc(S("hs_ps"), 1)

            def a_out(b):
                pe.wait_ge(S("hsh"), (b + 1) * NDH)
                pe.wait_ge(S("hsl"), (b + 1) * NDH)
                for t in range(NT):
                    last = three(P_(1)[:, t * D:(t + 1) * D], x_of(HS, t * P, P), w("w2", 0, D), range(NF1))
                last.then_inc(S("x1_ps"), 1)

            def f_gate(b, h):
                split_in(2, b)
                if h is not None:
                    pe.wait_ge(S("ql"), (h + 1) * KC)
                for t in range(NT):
                    last = three(P_(0)[:, t * 256:t * 256 + GA], x_of(XTF, t * P, P), w("ga", 0, GA), range(KC))
                last.then_inc(S("ga_ps"), 1)

            def f_lora_transposes(b):
                pe.wait_ge(S("am"), b + 1)
                for k in range(2 * NT):
                    last = nc.tensor.transpose(T_(1)[:, k * P:(k + 1) * P], am[:, k * P:(k + 1) * P], ident)
                last.then_inc(S("amT"), 1)

            def f_base(b, u):
                if u == 0 and not is0(b):
                    pe.wait_ge(S("x2"), b * NT)
                if u >= 2:
                    pe.wait_ge(S("hid"), b * NDF + u - 1)
                for k in range(2):
                    three(I_(u % 2)[:, k * T:(k + 1) * T], w("wi", (2 * u + k) * P), x_of(XTF), range(KC),
                          start=k == 0, stop=False, skip_group_check=True)

            def f_lora(b, u, which, signal):
                for k in range(2):
                    f = 2 * u + k
                    for q, (x, y) in enumerate(((0, 0), (1, 0), (0, 1))):
                        last = mm(I_(u % 2)[:, k * T:(k + 1) * T], (WH, WL)[x]["lb"][:, 0, f * P:(f + 1) * P],
                                  AT[y][:, which, :], start=False, stop=q == 2, skip_group_check=True)
                last.then_inc(S(signal), 1)

            def f_first(b, u):
                if u == 0:
                    pe.wait_ge(S("ath"), b + 1)
                    pe.wait_ge(S("atl"), b + 1)
                f_lora(b, u, 0, "first_ps")

            def f_second(b, u):
                pe.wait_ge(S("r1"), b * NDF + u + 1)
                f_lora(b, u, 1, "second_ps")

            def f_out(b, t, passes=range(3)):
                if t == 0:
                    if is0(b):
                        pe.wait_ge(S("split_h"), 7)
                        pe.wait_ge(S("wo_low"), 1)
                        pe.wait_ge(S("crow"), 1)
                    pe.wait_ge(S("hidh"), (b + 1) * NDF)
                    pe.wait_ge(S("hidl"), (b + 1) * NDF)
                last = three(I_(0)[:, t * D:(t + 1) * D], x_of((HH, HL), t * P, P), w("wo", 0, D), range(NFF), passes)
                if t == NT - 1 and 2 in passes:
                    last.then_inc(S("x2_ps"), 1)

            def c_scores(b):
                pe.wait_ge(S("kvc"), (b + 1) * 32)
                split_in(3, b)
                for t in range(NT):
                    last = three(T_(0)[:, t * KEYS:(t + 1) * KEYS], x_of(XTC, t * P, P), x_of(G, 0, KEYS), range(KC))
                last.then_inc(S("sc1_ps"), 1)

            def c_transpose(b):
                pe.wait_ge(S("ex1"), b + 1)
                nc.tensor.transpose(T_(1)[:, 0:P], sc1[:, :], ident).then_inc(S("ex1T"), 1)

            def c_attend(b):
                pe.wait_ge(S("eh"), b + 1)
                pe.wait_ge(S("el"), b + 1)
                for t in range(NT):
                    rows = slice(t * KEYS, (t + 1) * KEYS)
                    for q, (x, y) in enumerate(((0, 0), (1, 0), (0, 1))):
                        last = mm(T_(t)[:, 0:D], ET[x][rows, 0, :], V1[y][rows, :], start=q == 0, stop=q == 2)
                last.then_inc(S("p1"), 1)

            def c_linear(b):
                split_in(4, b)
                for t in range(NT):
                    last = three(T_(0)[:, t * D:(t + 1) * D], x_of(XTD, t * P, P), w("wc", 0, D), range(KC))
                last.then_inc(S("x4_ps"), 1)

            def constant_row():
                pe.wait_ge(S("ld_wo"), 16)
                pe.wait_ge(S("gb_ready"), 1)
                for f in range(NFF):
                    last = mm(T_(0)[:, 0:D], cols[:, BI + f:BI + f + 1].broadcast_to([P, P]),
                              STG["wo"][:, f * D:(f + 1) * D], start=f == 0, stop=f == NFF - 1)
                last.then_inc(S("crow_ps"), 1)

            def body(a, f, c, h):
                A_, F_, C_, H_ = (v is not None for v in (a, f, c, h))
                if F_:
                    f_lora_transposes(f)
                if A_:
                    a_scores(a, 0)
                    a_scores(a, 1)
                if C_:
                    c_scores(c)
                if F_:
                    f_first(f, 0)
                    f_first(f, 1)
                if F_:
                    f_second(f, 0)
                if C_:
                    c_transpose(c)
                if A_:
                    a_scores(a, 2)
                if F_:
                    f_second(f, 1)
                if A_:
                    a_attend(a, 0)
                    a_scores(a, 3)
                if F_:
                    f_base(f, 2)
                if C_:
                    c_attend(c)
                if A_:
                    a_attend(a, 1)
                if F_:
                    f_first(f, 2)
                    f_base(f, 3)
                    f_second(f, 2)
                    f_first(f, 3)
                if H_:
                    if C_:
                        pe.wait_ge(S("x3"), (c + 1) * NT)
                    transposes(1, h, T_(1))
                if A_:
                    if is0(a):
                        pe.wait_ge(S("split_h"), 3)
                        pe.wait_ge(S("split_l"), 3)
                    a_hidden(a, 0)
                    a_hidden(a, 1)
                if H_:
                    a_queries(h)
                if F_:
                    f_second(f, 3)
                if H_:
                    a_row_scores(h, 0)
                if A_:
                    a_out(a)
                if C_:
                    transposes(4, c, T_(0))
                if F_:
                    f_out(f, 0)
                if H_:
                    a_row_scores(h, 1)
                if F_:
                    f_out(f, 1, (0,))
                if A_:
                    if is0(a):
                        constant_row()
                    transposes(2, a, T_(1))
                if F_:
                    f_out(f, 1, (1, 2))
                if C_:
                    c_linear(c)
                if H_:
                    a_max_transposes(h)
                if A_:
                    if is0(a):
                        pe.wait_ge(S("split_h"), 5)
                        pe.wait_ge(S("split_l"), 5)
                    f_gate(a, h)
                    f_base(a, 0)
                    f_base(a, 1)
                if F_:
                    if C_:
                        pe.wait_ge(S("x4"), c + 1)
                    transposes(3, f, T_(0))

            pe.wait_ge(S("ld_a1"), 16)
            for m in range(KC):
                for k in range(2):
                    last = mm(I_(0)[:, m * P:(m + 1) * P], a1[:, k * D + m * P:k * D + (m + 1) * P],
                              a1[:, CTX + k * P:CTX + (k + 1) * P], start=k == 0, stop=k == 1)
            last.then_inc(S("proj"), 1)
            pe.wait_ge(S("ld_kept"), 16)
            transposes(1, 0, T_(1))
            pe.wait_ge(S("split_h"), 1)
            pe.wait_ge(S("split_l"), 1)
            a_queries(0)
            pe.wait_ge(S("ld_kvw"), 16)

            def values(bank, at):
                for b in range(BATCH):
                    for k in range(2):
                        o = CTXD + k * 2 * P + b * P
                        last = mm(bank[:, b * D:(b + 1) * D], kvw[:, o:o + P], kvw[:, at + k * D:at + (k + 1) * D],
                                  start=k == 0, stop=k == 1)
                return last

            values(I_(1), WV0).then_inc(S("proj"), 1)
            a_row_scores(0, 0)
            values(T_(0), WV1).then_inc(S("proj"), 1)
            a_row_scores(0, 1)
            for m in range(KC):
                for k in range(2):
                    last = mm(P_(1)[:, m * P:(m + 1) * P], kvw[:, WK1 + k * D + m * P:WK1 + k * D + (m + 1) * P],
                              a1[:, CTX + k * P:CTX + (k + 1) * P], start=k == 0, stop=k == 1)
            last.then_inc(S("proj"), 1)
            pe.wait_ge(S("kt1"), 1)
            a_max_transposes(0)
            pe.wait_ge(S("v1"), 1)
            pe.wait_ge(S("kt0"), 1)
            pe.wait_ge(S("ld_passing"), 16)
            for m in range(KC):
                for k in range(KC):
                    last = mm(I_(0)[:, m * P:(m + 1) * P], wq1t[:, k * D + m * P:k * D + (m + 1) * P],
                              kt1[:, k * P:(k + 1) * P], start=k == 0, stop=k == 1)
            last.then_inc(S("g_ps"), 1)
            for k in range(KC):
                last = mm(T_(0)[:, 0:P], cols[:, BQ1 + k:BQ1 + k + 1].broadcast_to([P, P]), kt1[:, k * P:(k + 1) * P],
                          start=k == 0, stop=k == 1)
            last.then_inc(S("gb_ps"), 1)
            pe.wait_ge(S("ind"), 1)
            body(0, None, None, 1)
            pe.wait_ge(S("split_h"), 6)
            pe.wait_ge(S("split_l"), 6)
            body(1, 0, None, 2)
            pe.wait_ge(S("split_h"), 8)
            pe.wait_ge(S("split_l"), 7)
            with pe.Fori(2, NBLK - 1) as i:
                body(i, i - 1, i - 2, i + 1)
            body(NBLK - 1, NBLK - 2, NBLK - 3, None)
            body(None, NBLK - 1, NBLK - 2, None)
            body(None, None, NBLK - 1, None)

        @block.scalar
        def _(act):
            A = nc.scalar.activation

            def normalise(j, b, src):
                act.wait_ge(S(f"ln{j}_nmr"), b + 1)
                for t in range(NT):
                    A(XN[j][:, t, :], src[:, t, :], ACT.Identity, scale=lnst[j][4][:, t:t + 1],
                      bias=lnst[j][5][:, t:t + 1]).then_inc(S(f"ln{j}_xh"), 1)

            def high(j, b, dst, bank):
                act.wait_ge(S(f"ln{j}_T"), b + 1)
                A(dst[0], bank.rearrange("p (c n) -> p c n", c=KC), ACT.Identity).then_inc(S(f"ln{j}_h"), 1)

            def queries(b):
                act.wait_ge(S("q_ps"), b + 1)
                for m in range(KC):
                    A(QU[0][:, m, :], P_(0)[:, m * T:(m + 1) * T], ACT.Identity,
                      bias=cols[:, BQ + m:BQ + m + 1]).then_inc(S("qh"), 1)

            def maxima(b):
                act.wait_ge(S("mxT_ps"), b + 1)
                A(mxT[:, :], P_(1)[0:HEADS, 0:T], ACT.Identity).then_inc(S("mxT"), 1)

            def exps(b, d):
                act.wait_ge(S("sc"), b * DPAIRS + d + 1)
                A(EX[:, 2 * d:2 * d + 2, :], S_(d % 2).rearrange("p (k n) -> p k n", k=2), ACT.Exp,
                  scale=SCALE).then_inc(S("ex"), 1)

            def attended(b, m):
                act.wait_ge(S("o32"), b * KC + m + 1)
                A(OA[0][:, m, :], O32[:, m, :], ACT.Identity).then_inc(S("oh"), 1)

            def hidden(b, u):
                act.wait_ge(S("hs_ps"), b * NDH + u + 1)
                for k in range(2):
                    c = 2 * u + k
                    last = A(HS32[:, c, :], S_(u)[:, k * T:(k + 1) * T], ACT.Relu, bias=cols[:, B1 + c:B1 + c + 1])
                last.then_inc(S("hs"), 1)

            def hidden_high(b, u):
                act.wait_ge(S("hs"), b * NDH + u + 1)
                A(HS[0][:, 2 * u:2 * u + 2, :], HS32[:, 2 * u:2 * u + 2, :], ACT.Identity).then_inc(S("hsh"), 1)

            def sorted_exps(b):
                act.wait_ge(S("srtd"), b + 1)
                A(srte[:, :], srtd[:, :], ACT.Exp).then_inc(S("srte"), 1)

            def lora_high(b):
                act.wait_ge(S("amT"), b + 1)
                A(AT[0], T_(1).rearrange("p (c n) -> p c n", c=2), ACT.Identity).then_inc(S("ath"), 1)

            def first_relu(b, u):
                act.wait_ge(S("first_ps"), b * NDF + u + 1)
                for k in range(2):
                    f = 2 * u + k
                    last = A(R1[:, f, :], I_(u % 2)[:, k * T:(k + 1) * T], ACT.Relu, bias=cols[:, BI + f:BI + f + 1])
                last.then_inc(S("r1"), 1)

            def sum_high(b, u):
                act.wait_ge(S("hid"), b * NDF + u + 1)
                A(HH[:, 2 * u:2 * u + 2, :], R1[:, 2 * u:2 * u + 2, :], ACT.Identity).then_inc(S("hidh"), 1)

            def weights_exp(b):
                act.wait_ge(S("sc1"), b + 1)
                A(sc1[:, :], sc1[:, :], ACT.Exp).then_inc(S("ex1"), 1)

            def weights_high(b):
                act.wait_ge(S("ex1T"), b + 1)
                A(ET[0][:, 0, :], T_(1)[:, 0:P], ACT.Identity).then_inc(S("eh"), 1)

            def store(b):
                act.wait_ge(S("x4"), b + 1)
                act.dma_start(out_v[b], X4).then_inc(S("stored"), 16)

            def body(a, f, c, h):
                A_, F_, C_, H_ = (v is not None for v in (a, f, c, h))
                if F_:
                    lora_high(f)
                if A_:
                    exps(a, 0)
                    exps(a, 1)
                if F_:
                    first_relu(f, 0)
                if C_:
                    weights_exp(c)
                if F_:
                    first_relu(f, 1)
                if C_:
                    weights_high(c)
                if A_:
                    exps(a, 2)
                if F_:
                    sum_high(f, 0)
                if A_:
                    exps(a, 3)
                if H_:
                    normalise(1, h, XIN)
                if F_:
                    sum_high(f, 1)
                    first_relu(f, 2)
                if A_:
                    attended(a, 0)
                    attended(a, 1)
                if F_:
                    first_relu(f, 3)
                if H_:
                    high(1, h, XTA, T_(1))
                if is0(a):
                    split("ga")
                    split("wi")
                    split("lb")
                if A_:
                    hidden(a, 0)
                    hidden_high(a, 0)
                    hidden(a, 1)
                    hidden_high(a, 1)
                if H_:
                    queries(h)
                if is0(a):
                    split("wo")
                if F_:
                    sum_high(f, 2)
                    sum_high(f, 3)
                if C_:
                    normalise(4, c, X3)
                    high(4, c, XTD, T_(0))
                if A_:
                    normalise(2, a, XMID)
                    high(2, a, XTF, T_(1))
                if H_:
                    maxima(h)
                if F_:
                    normalise(3, f, X2)
                if A_:
                    sorted_exps(a)
                if F_:
                    high(3, f, XTC, T_(0))
                if C_:
                    store(c)

            def split(n):
                act.wait_ge(S("ld_" + n), 16)
                if n == "wc":
                    act.wait_ge(S("wc_sum"), 1)
                A(wh[n][:, :], STG[n][:, :], ACT.Identity).then_inc(S("split_h"), 1)

            act.wait_ge(S("kt0"), 1)
            A(kt0_h[:, :], kt0[:, :], ACT.Identity).then_inc(S("kt0_h"), 1)
            normalise(1, 0, XIN)
            split("wq")
            high(1, 0, XTA, T_(1))
            act.wait_ge(S("ld_kept"), 16)
            queries(0)
            split("w1")
            act.wait_ge(S("ld_ind"), 16)
            A(ks[3 * PW:SROWS, :], ind[3 * PW:SROWS, 0:KV_S], ACT.Identity).then_inc(S("ind"), 1)
            act.wait_ge(S("v1"), 1)
            A(v1_h[:, :], v1[:, :], ACT.Identity).then_inc(S("v1_ready"), 1)
            maxima(0)
            act.wait_ge(S("g_ps"), 1)
            A(g_h[:, :], I_(0)[:, 0:KC * P], ACT.Identity).then_inc(S("g_ready"), 1)
            act.wait_ge(S("gb_ps"), 1)
            A(gb[:, :], T_(0)[:, 0:P], ACT.Identity).then_inc(S("gb_ready"), 1)
            split("w2")
            body(0, None, None, 1)
            split("wc")
            act.wait_ge(S("kvc_stored"), 16 * 7)
            act.wait_ge(S("wo_low"), 1)
            body(1, 0, None, 2)
            with act.Fori(2, NBLK - 1) as i:
                body(i, i - 1, i - 2, i + 1)
            body(NBLK - 1, NBLK - 2, NBLK - 3, None)
            body(None, NBLK - 1, NBLK - 2, None)
            body(None, None, NBLK - 1, None)

        @block.vector
        def _(dve):
            V = nc.vector
            SUB, ADD, MULT, MAX = ALU.subtract, ALU.add, ALU.mult, ALU.max

            def norm_stats(j, b, src):
                st, mv, ve, nm = lnst[j][:4]
                for t in range(NT):
                    V.bn_stats(r3(st, NT)[:, t, :], src[:, t, :]).then_inc(S(f"ln{j}_st"), 1)
                even, odd, both = r3(st, NT)[:, :, 0:3], r3(st, NT)[:, :, 3:6], r3(mv, 3)
                dve.wait_ge(S(f"ln{j}_st"), (b + 1) * NT)
                V.tensor_tensor(both[:, 0, :], even[:, :, 1], odd[:, :, 1], ADD).then_inc(S(f"ln{j}_mv"), 1)
                V.tensor_tensor(both[:, 1, :], even[:, :, 1], odd[:, :, 1], SUB).then_inc(S(f"ln{j}_mv"), 1)
                V.tensor_tensor(both[:, 2, :], even[:, :, 2], odd[:, :, 2], ADD).then_inc(S(f"ln{j}_mv"), 1)
                dve.wait_ge(S(f"ln{j}_mv"), b * 5 + 3)
                V.tensor_scalar(nm[:, :], both[:, 0, :], -0.5, None, MULT).then_inc(S(f"ln{j}_ve"), 1)
                V.tensor_tensor(both[:, 1, :], both[:, 1, :], both[:, 1, :], MULT).then_inc(S(f"ln{j}_mv"), 1)
                V.tensor_scalar(both[:, 2, :], both[:, 2, :], 1.0 / D, EPS, MULT, ADD).then_inc(S(f"ln{j}_mv"), 1)
                dve.wait_ge(S(f"ln{j}_mv"), b * 5 + 5)
                V.scalar_tensor_tensor(out=ve[:, :], in0=both[:, 1, :], scalar=0.25, in1=both[:, 2, :],
                                       op0=MULT, op1=ADD).then_inc(S(f"ln{j}_ve"), 1)

            def low(j, b, dst, bank):
                dve.wait_ge(S(f"ln{j}_h"), b + 1)
                V.tensor_tensor(dst[1], bank.rearrange("p (c n) -> p c n", c=KC), as32(dst[0]), SUB).then_inc(
                    S(f"ln{j}_l"), 1)

            def queries_low(b):
                dve.wait_ge(S("qh"), (b + 1) * KC)
                for m in range(KC):
                    V.scalar_tensor_tensor(out=QU[1][:, m, :], in0=P_(0)[:, m * T:(m + 1) * T],
                                           scalar=cols[:, BQ + m:BQ + m + 1], in1=as32(QU[0][:, m, :]),
                                           op0=ADD, op1=SUB).then_inc(S("ql"), 1)

            def row_max(b, t):
                dve.wait_ge(S("row_sc"), b * NT + t + 1)
                V.reduce_max(MX[:, t, :], psS[:, :].rearrange("p (h k) -> p h k", h=HEADS), AX.X).then_inc(S("mx"), 1)

            def attended(b, m):
                dve.wait_ge(S("pv"), b * KC + m + 1)
                V.reciprocal(REC[:, m, :], P_(m)[:, T:2 * T]).then_inc(S("rec"), 1)
                dve.wait_ge(S("rec"), b * KC + m + 1)
                V.tensor_tensor(O32[:, m, :], P_(m)[:, 0:T], REC[:, m, :], MULT).then_inc(S("o32"), 1)

            def first_residual(b):
                dve.wait_ge(S("x1_ps"), b + 1)
                dve.wait_ge(S("xres"), b + 1)
                if not is0(b):
                    dve.wait_ge(S("xg"), b)
                V.tensor_tensor(xmid[:, :], P_(1), xr[:, :], ADD).then_inc(S("x1"), 1)

            def experts(b):
                lg3, srt3, idx3, idxf3 = (r3(t, NT) for t in (lg, srt, idx, idxf))
                ga3 = P_(0).rearrange("p (t n) -> p t n", t=NT)
                dve.wait_ge(S("ga_ps"), b + 1)
                V.tensor_tensor(lg3, ga3[:, :, EXPERTS * RANK:GA], gbrow.unsqueeze(1).broadcast_to([P, NT, EXPERTS]),
                                ADD).then_inc(S("lg"), 1)
                dve.wait_ge(S("lg"), b + 1)
                V.tensor_copy(gnum[:, :], lg3[:, :, 0])
                for t in range(NT):
                    V.max(srt3[:, t, :], lg3[:, t, :]).then_inc(S("srt"), 1)
                dve.wait_ge(S("srt"), (b + 1) * NT)
                V.tensor_tensor(r3(srtd, NT), srt3, srt3[:, :, 0:1].broadcast_to([P, NT, EXPERTS]), SUB).then_inc(
                    S("srtd"), 1)
                for t in range(NT):
                    V.max_index(idx3[:, t, :], srt3[:, t, :], lg3[:, t, :]).then_inc(S("idx"), 1)
                dve.wait_ge(S("idx"), (b + 1) * NT)
                V.tensor_copy(idxf[:, :], idx[:, :]).then_inc(S("idxf"), 1)
                dve.wait_ge(S("idxf"), b + 1)
                for q, at in ((0, 0), (1, 2 * T)):
                    for t in range(NT):
                        V.scalar_tensor_tensor(out=am[:, at + t * P:at + (t + 1) * P], in0=eid,
                                               scalar=idxf3[:, t, q:q + 1], in1=ga3[:, t, 0:P],
                                               op0=ALU.is_equal, op1=MULT).then_inc(S("masked"), 1)
                dve.wait_ge(S("masked"), (b + 1) * 2 * NT)
                V.tensor_tensor(am[:, T:2 * T], am[:, 2 * T:3 * T], am[:, 0:T], SUB).then_inc(S("am"), 1)

            def gates(b):
                dve.wait_ge(S("srte"), b + 1)
                e3 = r3(srte, NT)
                V.reduce_sum(gsum[:, :], e3, AX.X).then_inc(S("gsum"), 1)
                V.tensor_tensor(gnum[:, :], e3[:, :, 0], e3[:, :, 1], ADD).then_inc(S("gsum"), 1)
                dve.wait_ge(S("gsum"), (b + 1) * 2)
                V.reciprocal(grec[:, :], gsum[:, :]).then_inc(S("grec"), 1)
                dve.wait_ge(S("grec"), b + 1)
                V.tensor_tensor(gate[:, :], gnum[:, :], grec[:, :], MULT).then_inc(S("gate"), 1)

            def lora_low(b):
                dve.wait_ge(S("ath"), b + 1)
                V.tensor_tensor(AT[1], T_(1).rearrange("p (c n) -> p c n", c=2), as32(AT[0]), SUB).then_inc(S("atl"), 1)

            def hidden_sum(b, u):
                dve.wait_ge(S("second_ps"), b * NDF + u + 1)
                for k in range(2):
                    f = 2 * u + k
                    last = V.scalar_tensor_tensor(out=R1[:, f, :], in0=I_(u % 2)[:, k * T:(k + 1) * T],
                                                  scalar=nbi[:, f:f + 1], in1=R1[:, f, :], op0=MAX, op1=ADD)
                last.then_inc(S("hid"), 1)

            def second_residual(b):
                dve.wait_ge(S("x2_ps"), b + 1)
                dve.wait_ge(S("xg"), b + 1)
                for t in range(NT):
                    V.scalar_tensor_tensor(out=X2[:, t, :], in0=I_(0)[:, t * D:(t + 1) * D], scalar=gate[:, t:t + 1],
                                           in1=XG[:, t, :], op0=MULT, op1=ADD).then_inc(S("x2"), 1)

            def weights_shift(b):
                dve.wait_ge(S("sc1_ps"), b + 1)
                V.tensor_tensor(SC1, T_(0)[:, 0:NT * KEYS].rearrange("p (t k) -> p t k", t=NT),
                                gbcur[:, :].unsqueeze(1).broadcast_to([P, NT, KEYS]), ADD).then_inc(S("sc1b"), 1)
                dve.wait_ge(S("sc1b"), b + 1)
                V.reduce_max(mx1[:, :], SC1, AX.X).then_inc(S("mx1"), 1)
                dve.wait_ge(S("mx1"), b + 1)
                V.tensor_tensor(SC1, SC1, mx1[:, :].unsqueeze(2).broadcast_to([P, NT, KEYS]), SUB).then_inc(
                    S("sc1"), 1)

            def weights_sums(b):
                dve.wait_ge(S("ex1"), b + 1)
                V.reduce_sum(sum1[:, :], SC1, AX.X).then_inc(S("sum1"), 1)
                dve.wait_ge(S("sum1"), b + 1)
                V.reciprocal(rec1[:, :], sum1[:, :]).then_inc(S("rec1"), 1)

            def weights_low(b):
                dve.wait_ge(S("eh"), b + 1)
                V.tensor_tensor(ET[1][:, 0, :], T_(1)[:, 0:P], as32(ET[0][:, 0, :]), SUB).then_inc(S("el"), 1)

            def third_residual(b):
                dve.wait_ge(S("p1"), b + 1)
                dve.wait_ge(S("rec1"), b + 1)
                for t in range(NT):
                    V.scalar_tensor_tensor(out=X3[:, t, :], in0=T_(t)[:, 0:D], scalar=rec1[:, t:t + 1],
                                           in1=X2[:, t, :], op0=MULT, op1=ADD).then_inc(S("x3"), 1)

            def fourth_residual(b):
                dve.wait_ge(S("x4_ps"), b + 1)
                dve.wait_ge(S("stored"), (b + 1) * 16)
                V.tensor_tensor(x4[:, :], T_(0), x3[:, :], ADD).then_inc(S("x4"), 1)

            def body(a, f, c, h):
                A_, F_, C_, H_ = (v is not None for v in (a, f, c, h))
                if F_:
                    lora_low(f)
                if C_:
                    weights_shift(c)
                if H_:
                    dve.wait_ge(S("x_in"), (h + 1) * 16)
                    norm_stats(1, h, XIN)
                if C_:
                    weights_sums(c)
                    weights_low(c)
                if F_:
                    hidden_sum(f, 0)
                    hidden_sum(f, 1)
                if A_:
                    attended(a, 0)
                if C_:
                    third_residual(c)
                if A_:
                    attended(a, 1)
                if H_:
                    low(1, h, XTA, T_(1))
                if F_:
                    hidden_sum(f, 2)
                if C_:
                    dve.wait_ge(S("x3"), (c + 1) * NT)
                    norm_stats(4, c, X3)
                if F_:
                    hidden_sum(f, 3)
                if is0(a):
                    split("ga")
                    split("wi")
                    split("lb")
                if H_:
                    queries_low(h)
                if H_:
                    row_max(h, 0)
                if A_:
                    first_residual(a)
                    dve.wait_ge(S("x1"), a + 1)
                    norm_stats(2, a, XMID)
                if C_:
                    low(4, c, XTD, T_(0))
                if H_:
                    row_max(h, 1)
                if A_:
                    low(2, a, XTF, T_(1))
                if F_:
                    second_residual(f)
                    dve.wait_ge(S("x2"), (f + 1) * NT)
                    norm_stats(3, f, X2)
                if C_:
                    fourth_residual(c)
                if A_:
                    experts(a)
                    gates(a)
                if F_:
                    low(3, f, XTC, T_(0))

            def split(n):
                dve.wait_ge(S("split_h"), SPLIT_ORDER.index(n) + 1)
                V.tensor_tensor(wl[n][:, :], STG[n][:, :], as32(wh[n][:, :]), SUB).then_inc(S("split_l"), 1)

            V.memset(mhalf[:, :], -0.5).then_inc(S("mhalf"), 1)
            dve.wait_ge(S("ld_kept"), 16)
            dve.wait_ge(S("proj"), 1)
            V.tensor_tensor(r3(kt0, KC), I_(0)[:, 0:KC * P].rearrange("p (m n) -> p m n", m=KC),
                            cols[:, BK0:BK0 + KC].unsqueeze(2).broadcast_to([P, KC, P]), ADD).then_inc(S("kt0"), 1)
            dve.wait_ge(S("x_in"), 16)
            norm_stats(1, 0, XIN)
            dve.wait_ge(S("kt0_h"), 1)
            V.tensor_tensor(kt0_l[:, :], kt0[:, :], as32(kt0_h[:, :]), SUB).then_inc(S("kt0_l"), 1)

            def block_diagonal(kb, kt, signal):
                for m in range(KC):
                    V.tensor_tensor(
                        kb[:, :].rearrange("p (b m h k) -> p b m h k", b=BATCH, m=KC, h=8)[:, :, m],
                        as32(kt[:, m * P:(m + 1) * P]).rearrange("p (b k) -> p b k", b=BATCH).unsqueeze(2).broadcast_to(
                            [P, BATCH, 8, KEYS]),
                        kmask.unsqueeze(1).unsqueeze(3).broadcast_to([P, BATCH, 8, KEYS]), MULT).then_inc(S(signal), 1)

            block_diagonal(kb_h, kt0_h, "kb_high")
            dve.wait_ge(S("kt0_l"), 1)
            block_diagonal(kb_l, kt0_l, "kb_low")

            split("wq")
            low(1, 0, XTA, T_(1))
            queries_low(0)
            dve.wait_ge(S("ld_passing"), 16)
            dve.wait_ge(S("proj"), 2)
            V.tensor_tensor(r3(v0, BATCH), I_(1).rearrange("p (b n) -> p b n", b=BATCH),
                            bvrow0.unsqueeze(1).broadcast_to([P, BATCH, D]), ADD).then_inc(S("v0"), 1)
            row_max(0, 0)
            dve.wait_ge(S("v0"), 1)
            V.tensor_tensor(r3(v0, BATCH), r3(v0, BATCH), vmask.unsqueeze(1).broadcast_to([P, BATCH, D]),
                            MULT).then_inc(S("v0_ready"), 1)
            dve.wait_ge(S("proj"), 3)
            V.tensor_tensor(r3(v1, BATCH), T_(0).rearrange("p (b n) -> p b n", b=BATCH),
                            bvrow1.unsqueeze(1).broadcast_to([P, BATCH, D]), ADD).then_inc(S("v1"), 1)
            row_max(0, 1)
            dve.wait_ge(S("proj"), 4)
            V.tensor_tensor(r3(kt1, KC), P_(1)[:, 0:KC * P].rearrange("p (m n) -> p m n", m=KC),
                            cols[:, BK1:BK1 + KC].unsqueeze(2).broadcast_to([P, KC, P]), ADD).then_inc(S("kt1"), 1)
            split("w1")
            V.tensor_scalar(nbi[:, :], cols[:, BI:BI + NFF], -1.0, None, MULT).then_inc(S("nbi"), 1)
            dve.wait_ge(S("v1_ready"), 1)
            V.tensor_tensor(v1_l[:, :], v1[:, :], as32(v1_h[:, :]), SUB).then_inc(S("v1_ready"), 1)
            dve.wait_ge(S("g_ready"), 1)
            V.tensor_tensor(g_l[:, :], I_(0)[:, 0:KC * P], as32(g_h[:, :]), SUB).then_inc(S("g_ready"), 1)
            split("w2")
            body(0, None, None, 1)
            dve.wait_ge(S("stored"), 16)
            dve.wait_ge(S("ld_wc"), 16)
            V.tensor_tensor(r3(STG["wc"], KC), r3(STG["wc"], KC),
                            late[:, D:2 * D].unsqueeze(1).broadcast_to([P, KC, D]), ADD).then_inc(S("wc_sum"), 1)
            dve.wait_ge(S("crow_ps"), 1)
            V.scalar_tensor_tensor(out=crow[:, :], in0=late[:, 0:D], scalar=2.0, in1=T_(0)[:, 0:D],
                                   op0=MULT, op1=ADD).then_inc(S("crow"), 1)
            split("wc")
            dve.wait_ge(S("nbi"), 1)
            dve.wait_ge(S("kvc_stored"), 16 * 7)
            body(1, 0, None, 2)
            with dve.Fori(2, NBLK - 1) as i:
                body(i, i - 1, i - 2, i + 1)
            body(NBLK - 1, NBLK - 2, NBLK - 3, None)
            body(None, NBLK - 1, NBLK - 2, None)
            body(None, None, NBLK - 1, None)

        @block.gpsimd
        def _(pool):
            G_ = nc.gpsimd

            def scale(j, b):
                _, _, ve, nm, rs, nmr = lnst[j]
                pool.wait_ge(S(f"ln{j}_ve"), (b + 1) * 2)
                G_.tensor_tensor(rs[:, :], ve[:, :], mhalf[:, :], ALU.pow).then_inc(S(f"ln{j}_rs"), 1)
                pool.wait_ge(S(f"ln{j}_rs"), b + 1)
                G_.tensor_tensor(nmr[:, :], nm[:, :], rs[:, :], ALU.mult).then_inc(S(f"ln{j}_nmr"), 1)

            def attended_low(b, m):
                pool.wait_ge(S("oh"), b * KC + m + 1)
                G_.tensor_tensor(OA[1][:, m, :], O32[:, m, :], as32(OA[0][:, m, :]), ALU.subtract).then_inc(S("ol"), 1)

            def hidden_low(b, u):
                pool.wait_ge(S("hsh"), b * NDH + u + 1)
                two = slice(2 * u, 2 * u + 2)
                G_.tensor_tensor(HS[1][:, two, :], HS32[:, two, :], as32(HS[0][:, two, :]), ALU.subtract).then_inc(
                    S("hsl"), 1)

            def sum_low(b, u):
                pool.wait_ge(S("hidh"), b * NDF + u + 1)
                two = slice(2 * u, 2 * u + 2)
                G_.tensor_tensor(HL[:, two, :], R1[:, two, :], as32(HH[:, two, :]), ALU.subtract).then_inc(
                    S("hidl"), 1)

            def gated(b):
                pool.wait_ge(S("gate"), b + 1)
                G_.tensor_tensor(XG, crow[:, :].unsqueeze(1).broadcast_to([P, NT, D]),
                                 gate[:, :].unsqueeze(2).broadcast_to([P, NT, D]), ALU.mult).then_inc(S("gc"), 1)
                pool.wait_ge(S("x1"), b + 1)
                pool.wait_ge(S("gc"), b + 1)
                G_.tensor_tensor(xg[:, :], xg[:, :], xmid[:, :], ALU.add).then_inc(S("xg"), 1)

            def residual(b):
                if not is0(b):
                    pool.wait_ge(S("x1"), b)
                pool.wait_ge(S("x_in"), (b + 1) * 16)
                G_.tensor_tensor(r3(xr, NT), XIN, b2row.unsqueeze(1).broadcast_to([P, NT, D]), ALU.add).then_inc(
                    S("xres"), 1)

            def body(a, f, c, h):
                A_, F_, C_, H_ = (v is not None for v in (a, f, c, h))
                if H_:
                    scale(1, h)
                if F_:
                    if is0(f):
                        pool.wait_ge(S("crow"), 1)
                    gated(f)
                    sum_low(f, 0)
                    sum_low(f, 1)
                if A_:
                    attended_low(a, 0)
                    attended_low(a, 1)
                if A_:
                    hidden_low(a, 0)
                    hidden_low(a, 1)
                if C_:
                    scale(4, c)
                if F_:
                    sum_low(f, 2)
                    sum_low(f, 3)
                if A_:
                    scale(2, a)
                if H_:
                    residual(h)
                if is0(a):
                    pool.wait_ge(S("split_h"), 7)
                    G_.tensor_tensor(wl["wo"][:, :], STG["wo"][:, :], as32(wh["wo"][:, :]), ALU.subtract).then_inc(
                        S("wo_low"), 1)
                if F_:
                    scale(3, f)

            pool.wait_ge(S("mhalf"), 1)
            scale(1, 0)
            pool.wait_ge(S("ld_kept"), 16)
            residual(0)
            body(0, None, None, 1)
            body(1, 0, None, 2)
            with pool.Fori(2, NBLK - 1) as i:
                body(i, i - 1, i - 2, i + 1)
            body(NBLK - 1, NBLK - 2, NBLK - 3, None)
            body(None, NBLK - 1, NBLK - 2, None)
            body(None, None, NBLK - 1, None)


IN = ["x", "a1", "kept", "wq", "kvw", "passing", "ind", "w1", "w2", "ga", "lb", "late", "wi", "wo", "wc"]


def kernel(x, ctx_768, **w):
    import concourse.bacc as bacc
    from concourse.bass_utils import run_bass_kernel_spmd

    def rows(a):
        a = np.asarray(a)
        return a.reshape(-1, P, a.shape[1]).transpose(1, 0, 2).reshape(P, -1)

    def crows(a):
        a = np.asarray(a)
        return a.reshape(2, CK, a.shape[1]).transpose(1, 0, 2).reshape(CK, -1)

    def col(v):
        return np.asarray(v).reshape(-1, P).T

    def every(v):
        return np.broadcast_to(np.asarray(v)[None, :], (P, v.shape[0]))

    p, c, key = np.arange(P), np.arange(D), np.arange(KV_S)
    ind = np.zeros((HEADS, KV_S), np.float32)
    ind[2 * (key // P) + (key % P) // KEYS, key] = -1.0
    small = {
        "kmask": (p[:, None] // HD == np.arange(8)[None, :]).astype(np.float32),
        "ident": np.eye(P, dtype=np.float32),
        "vmask": (p[:, None] // KEYS == (c[None, :] // HD) % 2).astype(np.float32),
        "ones_pair": (p[:, None] // KEYS == np.arange(PW)[None, :] // HD).astype(np.float32),
        "eid": np.broadcast_to((p // RANK).astype(np.float32)[None, :], (P, P)),
        "cols": np.concatenate([col(w[n]) for n in ("L0_xattn_bq", "L0_xattn_b1", "L0_ffn_bi", "L0_xattn_bk",
                                                    "L1_xattn_bk", "L1_xattn_bq")], axis=1),
        "b2row": every(w["L0_xattn_b2"]), "gbrow": every(w["L0_ffn_gate_b"]),
        "bvrow0": every(w["L0_xattn_bv"]), "bvrow1": every(w["L1_xattn_bv"]),
        "wq1t": rows(np.asarray(w["L1_xattn_Wq"]).T),
    }
    side = lambda parts: np.concatenate(parts, axis=1)
    ct = np.asarray(ctx_768).reshape(BATCH * KEYS, DC).T.reshape(2, CK, BATCH, KEYS).transpose(1, 0, 2, 3)
    arrays = {
        "x": np.asarray(x).reshape(BATCH * SEQ, D),
        "a1": side([crows(w["L0_xattn_Wk"]), ct.reshape(CK, -1)]),
        "kvw": side([crows(w["L0_xattn_Wv"]), crows(w["L1_xattn_Wk"]), crows(w["L1_xattn_Wv"]),
                     np.concatenate([ct, ct], axis=3).reshape(CK, -1)]),
        "kept": side([small[n] for n, _ in KEPT]),
        "passing": side([small[n] for n, _ in PASSING]),
        "late": side([every(w["L0_ffn_bo"]), np.concatenate([np.asarray(w["L1_ffn_disha"])] * 2, axis=0)]),
        "ind": ind,
        "wq": rows(w["L0_xattn_Wq"]), "w1": rows(w["L0_xattn_W1"]), "w2": rows(w["L0_xattn_W2"]),
        "ga": rows(np.concatenate([np.asarray(w["L0_ffn_lora_A"]).reshape(EXPERTS * RANK, D),
                                   np.asarray(w["L0_ffn_gate_w"])], axis=0).T),
        "lb": np.asarray(w["L0_ffn_lora_B"]).transpose(0, 2, 1).reshape(EXPERTS * RANK, DFF),
        "wi": rows(np.asarray(w["L0_ffn_wi"]).T), "wo": rows(np.asarray(w["L0_ffn_wo"]).T),
        "wc": rows(np.asarray(w["L1_ffn_weight"]).T),
    }
    nc = bacc.Bacc("TRN2", target_bir_lowering=False, num_devices=1)
    io, feeds = {}, {}
    for n in IN:
        feeds[f"in_{n}"] = np.ascontiguousarray(arrays[n])
        io[n] = nc.dram_tensor(f"in_{n}", feeds[f"in_{n}"].shape, F32, kind="ExternalInput").ap()
    io["out"] = nc.dram_tensor("out", (BATCH * SEQ, D), F32, kind="ExternalOutput").ap()
    build(nc, io)
    r = run_bass_kernel_spmd(nc, [feeds], core_ids=[0])
    return r.results[0]["out"].reshape(BATCH, SEQ, D)
```
